# Optimizing a Trainium2 kernel written in Bass

```python
import numpy as np
import jax
import jax.numpy as jnp

def _softmax(x, axis=-1):
    return jax.nn.softmax(x, axis=axis)

def _gelu(x):
    return jax.nn.gelu(x, approximate=True)

def _silu(x):
    return jax.nn.silu(x)

def _sigmoid(x):
    return jax.nn.sigmoid(x)

def _layernorm(x, axis=-1, eps=1e-05):
    m = jnp.mean(x, axis=axis, keepdims=True)
    v = jnp.var(x, axis=axis, keepdims=True)
    return (x - m) / jnp.sqrt(v + eps)

def _scatter_add(tgt, idx, src, axis=0):
    return tgt.at[idx].add(src)

def _segment_sum(src, seg, n):
    return jax.ops.segment_sum(src, seg, n)
kernel_name = 'mk_gnn_preln_d4_gnn_r32_71feef'

def setup_inputs(seed: int=0):
    np.random.seed(seed)
    _w = jnp.asarray

    def _rec_inputs():
        import jax
        import jax.numpy as jnp
        _gk = jax.random.key(seed)
        x = -0.0005207 + 1.001 * jax.random.normal(jax.random.fold_in(_gk, 1), (128, 512), jnp.float32)
        src = jax.random.randint(jax.random.fold_in(_gk, 2), (2048,), 0, 128, jnp.int32)
        dst = jax.random.randint(jax.random.fold_in(_gk, 3), (2048,), 0, 128, jnp.int32)
        _o = jnp.argsort(dst, stable=True)
        src = src[_o]
        dst = dst[_o]
        edge_type_8 = jax.random.randint(jax.random.fold_in(_gk, 13), (2048,), 0, 8, jnp.int32)
        edge_weight = jax.random.uniform(jax.random.fold_in(_gk, 14), (2048,), jnp.float32, 0.0, 0.999998)
        edge_weight1 = jax.random.uniform(jax.random.fold_in(_gk, 15), (2048, 1), jnp.float32, 0.0, 0.999996)
        return (x, src, dst, edge_type_8, edge_weight, edge_weight1)
    x, src, dst, edge_type_8, edge_weight, edge_weight1 = _rec_inputs()

    def _L0_gnn_setup():
        import jax, jax.numpy as jnp
        import numpy as np
        N = 128
        FEAT = 512
        HID = 256
        E = 4096
        key = jax.random.key(seed)
        ks = jax.random.split(key, 10)
        x = jax.random.normal(ks[0], (N, FEAT), dtype=jnp.float32)
        edge_index = jax.random.randint(ks[1], (2, E), 0, N)
        edge_attr = jax.random.uniform(ks[2], (E, 1), dtype=jnp.float32)
        Wk = jax.random.normal(ks[3], (FEAT, HID), dtype=jnp.float32) / np.sqrt(FEAT)
        Wq = jax.random.normal(ks[4], (FEAT, HID), dtype=jnp.float32) / np.sqrt(FEAT)
        Wv = jax.random.normal(ks[5], (FEAT, FEAT), dtype=jnp.float32) / np.sqrt(FEAT)
        Ek = jax.random.normal(ks[6], (2, HID), dtype=jnp.float32)
        Eq = jax.random.normal(ks[7], (2, HID), dtype=jnp.float32)
        Ev = jax.random.normal(ks[8], (2, FEAT), dtype=jnp.float32)
        idx_bias = jnp.full((1,), 0.5, dtype=jnp.float32)
        idx_mult = jnp.full((1,), 10.0, dtype=jnp.float32)
        return dict(x=x, edge_index=edge_index, edge_attr=edge_attr, Wk=Wk, Wq=Wq, Wv=Wv, Ek=Ek, Eq=Eq, Ev=Ev, idx_bias=idx_bias, idx_mult=idx_mult)
    _L0_gnn_all = _L0_gnn_setup()
    _L0_gnn_in = {k: v for k, v in _L0_gnn_all.items() if k in ('Wk', 'Wq', 'Wv', 'Ek', 'Eq', 'Ev', 'idx_bias', 'idx_mult')}
    del _L0_gnn_all

    def _L1_gnn_setup():
        import jax, jax.numpy as jnp
        import numpy as np
        N_NODES = 625
        N_EDGES = 10000
        D = 512
        NUM_RELS = 8
        NUM_BASES = 4

        def _rel_graph_conv(h, src, dst, etypes, norm, basis, comp, bias, loop_w, apply_relu):
            n = h.shape[0]
            hb = jnp.einsum('nd,bdo->bno', h, basis)
            coef = comp[etypes]
            m = coef[:, 0, None] * hb[0][src]
            for b in range(1, basis.shape[0]):
                m = m + coef[:, b, None] * hb[b][src]
            m = m * norm[:, None]
            agg = jax.ops.segment_sum(m, dst, num_segments=n)
            out = agg + bias + h @ loop_w
            if apply_relu:
                out = jax.nn.relu(out)
            return out
        key = jax.random.key(seed)
        ks = jax.random.split(key, 16)
        inp = {'emb': jax.random.normal(ks[0], (N_NODES, D), dtype=jnp.float32), 'src': jax.random.randint(ks[1], (N_EDGES,), 0, N_NODES), 'dst': jax.random.randint(ks[2], (N_EDGES,), 0, N_NODES), 'etypes': jax.random.randint(ks[3], (N_EDGES,), 0, NUM_RELS), 'edge_norm': jax.random.uniform(ks[4], (N_EDGES,), dtype=jnp.float32)}
        s = 1.0 / np.sqrt(D)
        inp['basis0'] = jax.random.normal(ks[5], (NUM_BASES, D, D), dtype=jnp.float32) * s
        inp['comp0'] = jax.random.normal(ks[6], (NUM_RELS, NUM_BASES), dtype=jnp.float32)
        inp['bias0'] = jnp.zeros((D,), dtype=jnp.float32)
        inp['loop0'] = jax.random.normal(ks[7], (D, D), dtype=jnp.float32) * s
        inp['basis1'] = jax.random.normal(ks[8], (NUM_BASES, D, D), dtype=jnp.float32) * s
        inp['comp1'] = jax.random.normal(ks[9], (NUM_RELS, NUM_BASES), dtype=jnp.float32)
        inp['bias1'] = jnp.zeros((D,), dtype=jnp.float32)
        inp['loop1'] = jax.random.normal(ks[10], (D, D), dtype=jnp.float32) * s
        return inp
    _L1_gnn_all = _L1_gnn_setup()
    _L1_gnn_in = {k: v for k, v in _L1_gnn_all.items() if k in ('basis0', 'comp0', 'bias0', 'loop0', 'basis1', 'comp1', 'bias1', 'loop1')}
    del _L1_gnn_all

    def _L2_gnn_setup():
        import jax, jax.numpy as jnp
        import numpy as np
        N_NODES = 3125
        N_EDGES = 100000
        IN_F = 512
        OUT_F = 512
        RANK = 64
        key = jax.random.key(seed)
        ks = jax.random.split(key, 8)
        inp = jax.random.normal(ks[0], (N_NODES, IN_F), dtype=jnp.float32)
        U = jax.random.normal(ks[1], (IN_F, RANK), dtype=jnp.float32) / np.sqrt(IN_F)
        s = jax.random.uniform(ks[2], (RANK,), dtype=jnp.float32)
        Vt = jax.random.normal(ks[3], (RANK, OUT_F), dtype=jnp.float32) / np.sqrt(RANK)
        bias = jax.random.normal(ks[4], (OUT_F,), dtype=jnp.float32) * 0.01
        edge_row = jax.random.randint(ks[5], (N_EDGES,), 0, N_NODES, dtype=jnp.int64 if jax.config.jax_enable_x64 else jnp.int32)
        edge_col = jax.random.randint(ks[6], (N_EDGES,), 0, N_NODES, dtype=jnp.int64 if jax.config.jax_enable_x64 else jnp.int32)
        edge_val = jax.random.uniform(ks[7], (N_EDGES,), dtype=jnp.float32)
        return {'input': inp, 'U': U, 's': s, 'Vt': Vt, 'bias': bias, 'edge_row': edge_row, 'edge_col': edge_col, 'edge_val': edge_val}
    _L2_gnn_all = _L2_gnn_setup()
    _L2_gnn_in = {k: v for k, v in _L2_gnn_all.items() if k in ('U', 's', 'Vt', 'bias')}
    del _L2_gnn_all

    def _L3_gnn_setup():
        import jax, jax.numpy as jnp
        import numpy as np
        N_NODES = 50000
        N_EDGES = 12500
        IN_DIM = 512
        OUT_DIM = 512
        key = jax.random.key(seed)
        k1, k2, k3, k4 = jax.random.split(key, 4)
        x = jax.random.normal(k1, (N_NODES, IN_DIM), dtype=jnp.float32)
        edge_index = jax.random.randint(k2, (2, N_EDGES), 0, N_NODES, dtype=jnp.int64)
        W = jax.random.normal(k3, (OUT_DIM, IN_DIM), dtype=jnp.float32) / np.sqrt(IN_DIM)
        b = jax.random.normal(k4, (OUT_DIM,), dtype=jnp.float32) * 0.01
        return {'x': x, 'edge_index': edge_index, 'W': W, 'b': b}
    _L3_gnn_all = _L3_gnn_setup()
    _L3_gnn_in = {k: v for k, v in _L3_gnn_all.items() if k in ('W', 'b')}
    del _L3_gnn_all
    return {'x': x, 'src': src, 'dst': dst, 'edge_type_8': edge_type_8, 'edge_weight': edge_weight, 'edge_weight1': edge_weight1, 'L0_gnn_Wk': _L0_gnn_in['Wk'], 'L0_gnn_Wq': _L0_gnn_in['Wq'], 'L0_gnn_Wv': _L0_gnn_in['Wv'], 'L0_gnn_Ek': _L0_gnn_in['Ek'], 'L0_gnn_Eq': _L0_gnn_in['Eq'], 'L0_gnn_Ev': _L0_gnn_in['Ev'], 'L0_gnn_idx_bias': _L0_gnn_in['idx_bias'], 'L0_gnn_idx_mult': _L0_gnn_in['idx_mult'], 'L1_gnn_basis0': _L1_gnn_in['basis0'], 'L1_gnn_comp0': _L1_gnn_in['comp0'], 'L1_gnn_bias0': _L1_gnn_in['bias0'], 'L1_gnn_loop0': _L1_gnn_in['loop0'], 'L1_gnn_basis1': _L1_gnn_in['basis1'], 'L1_gnn_comp1': _L1_gnn_in['comp1'], 'L1_gnn_bias1': _L1_gnn_in['bias1'], 'L1_gnn_loop1': _L1_gnn_in['loop1'], 'L2_gnn_U': _L2_gnn_in['U'], 'L2_gnn_s': _L2_gnn_in['s'], 'L2_gnn_Vt': _L2_gnn_in['Vt'], 'L2_gnn_bias': _L2_gnn_in['bias'], 'L3_gnn_W': _L3_gnn_in['W'], 'L3_gnn_b': _L3_gnn_in['b']}

def reference(x, src, dst, edge_type_8, edge_weight, edge_weight1, L0_gnn_Wk, L0_gnn_Wq, L0_gnn_Wv, L0_gnn_Ek, L0_gnn_Eq, L0_gnn_Ev, L0_gnn_idx_bias, L0_gnn_idx_mult, L1_gnn_basis0, L1_gnn_comp0, L1_gnn_bias0, L1_gnn_loop0, L1_gnn_basis1, L1_gnn_comp1, L1_gnn_bias1, L1_gnn_loop1, L2_gnn_U, L2_gnn_s, L2_gnn_Vt, L2_gnn_bias, L3_gnn_W, L3_gnn_b):
    import jax
    import jax.numpy as jnp

    def _L0_gnn_ref(x, edge_index, edge_attr, Wk, Wq, Wv, Ek, Eq, Ev, idx_bias, idx_mult):
        import jax, jax.numpy as jnp
        import numpy as np
        N = 128
        FEAT = 512
        HID = 256
        E = 4096
        n = x.shape[0]
        L = x.shape[-1]
        src, dst = (edge_index[0], edge_index[1])
        s = jax.nn.sigmoid((edge_attr - idx_bias) * idx_mult)
        w = jnp.concatenate([s, 1.0 - s], axis=-1)
        rk = w @ Ek
        rq = w @ Eq
        rv = w @ Ev
        k = x @ Wk
        q = x @ Wq
        v = x @ Wv
        A = 2.0 * (q @ k.T)
        edge_bias = jnp.sum(q[src] * rk, axis=-1) + jnp.sum(k[dst] * rq, axis=-1)
        A = A.at[src, dst].add(edge_bias)
        A = jax.nn.softmax(A / np.sqrt(L), axis=-1)
        M = A @ v
        M = M + jax.ops.segment_sum(A[src, dst][:, None] * rv, src, num_segments=n)
        return M

    def _L1_gnn_ref(emb, src, dst, etypes, edge_norm, basis0, comp0, bias0, loop0, basis1, comp1, bias1, loop1):
        import jax, jax.numpy as jnp
        import numpy as np
        N_NODES = 625
        N_EDGES = 10000
        D = 512
        NUM_RELS = 8
        NUM_BASES = 4

        def _rel_graph_conv(h, src, dst, etypes, norm, basis, comp, bias, loop_w, apply_relu):
            n = h.shape[0]
            hb = jnp.einsum('nd,bdo->bno', h, basis)
            coef = comp[etypes]
            m = coef[:, 0, None] * hb[0][src]
            for b in range(1, basis.shape[0]):
                m = m + coef[:, b, None] * hb[b][src]
            m = m * norm[:, None]
            agg = jax.ops.segment_sum(m, dst, num_segments=n)
            out = agg + bias + h @ loop_w
            if apply_relu:
                out = jax.nn.relu(out)
            return out
        h = _rel_graph_conv(emb, src, dst, etypes, edge_norm, basis0, comp0, bias0, loop0, True)
        h = _rel_graph_conv(h, src, dst, etypes, edge_norm, basis1, comp1, bias1, loop1, False)
        return h

    def _L2_gnn_ref(input, U, s, Vt, bias, edge_row, edge_col, edge_val):
        import jax, jax.numpy as jnp
        import numpy as np
        N_NODES = 3125
        N_EDGES = 100000
        IN_F = 512
        OUT_F = 512
        RANK = 64
        support = input @ U * s
        support = support @ Vt
        gathered = support[edge_col] * edge_val[:, None]
        output = jax.ops.segment_sum(gathered, edge_row, num_segments=input.shape[0])
        output = output + bias
        return jax.nn.relu(output)

    def _L3_gnn_ref(x, edge_index, W, b):
        import jax, jax.numpy as jnp
        import numpy as np
        N_NODES = 50000
        N_EDGES = 12500
        IN_DIM = 512
        OUT_DIM = 512
        n = x.shape[0]
        loops = jnp.arange(n, dtype=edge_index.dtype)
        row = jnp.concatenate([edge_index[0], loops])
        col = jnp.concatenate([edge_index[1], loops])
        deg = jax.ops.segment_sum(jnp.ones(row.shape[0], dtype=x.dtype), row, num_segments=n)
        dis = jax.lax.rsqrt(deg)
        norm = dis[row] * dis[col]
        h = x @ W.T + b
        out = jax.ops.segment_sum(norm[:, None] * h[row], col, num_segments=n)
        return jax.nn.relu(out)
    edge_index = jnp.stack([src, dst])
    h = jnp.maximum(_layernorm(x, axis=-1), 0.0)
    x = x + _L0_gnn_ref(h, edge_index, edge_weight1, L0_gnn_Wk, L0_gnn_Wq, L0_gnn_Wv, L0_gnn_Ek, L0_gnn_Eq, L0_gnn_Ev, L0_gnn_idx_bias, L0_gnn_idx_mult)
    h = jnp.maximum(_layernorm(x, axis=-1), 0.0)
    x = x + _L1_gnn_ref(h, src, dst, edge_type_8, edge_weight, L1_gnn_basis0, L1_gnn_comp0, L1_gnn_bias0, L1_gnn_loop0, L1_gnn_basis1, L1_gnn_comp1, L1_gnn_bias1, L1_gnn_loop1)
    h = jnp.maximum(_layernorm(x, axis=-1), 0.0)
    x = x + _L2_gnn_ref(h, L2_gnn_U, L2_gnn_s, L2_gnn_Vt, L2_gnn_bias, src, dst, edge_weight)
    h = jnp.maximum(_layernorm(x, axis=-1), 0.0)
    x = x + _L3_gnn_ref(h, edge_index, L3_gnn_W, L3_gnn_b)
    return x

_drawn_inputs = setup_inputs


def setup_inputs(seed=0):
    import zlib

    import numpy as np

    out = dict(_drawn_inputs(seed))
    spreads = {'L1_gnn_bias0': (0.0, 0.1), 'L1_gnn_bias1': (0.0, 0.8)}
    factors = {'L2_gnn_bias': 64.0, 'L3_gnn_W': 3.244, 'L3_gnn_b': 64.0}
    for name, (base, spread) in spreads.items():
        noise = np.random.default_rng([zlib.crc32(name.encode()), seed]).standard_normal(out[name].shape)
        drawn = base * np.exp(spread * noise) if base else spread * noise
        out[name] = jnp.asarray(drawn.astype(out[name].dtype))
    for name, factor in factors.items():
        out[name] = (out[name] * factor).astype(out[name].dtype)
    return out
```

```python
from contextlib import ExitStack

import concourse.bass as bass
from concourse import mybir

ALU = mybir.AluOpType
ACT = mybir.ActivationFunctionType
AX_X = mybir.AxisListType.X
F32 = mybir.dt.float32
F32R = mybir.dt.float32r
I32 = mybir.dt.int32

P = 128
D = 512
DC = D // P
EC = 16
RELS = 8
BASES = 4
HID = 256
RANK = 64
LN_EPS = 1e-5
SCALE = float(D) ** -0.5
RING = 4

NORM, W1, EK, EQ, IDXB, IDXM, COMP0, COMP1, S2, SMALLS = 0, 16, 32, 36, 40, 41, 42, 74, 106, 107


def gnn_stack(nc: bass.Bass, x_d, ints_d, smalls_d, biases_d, ev_d, wkq_d, wv_d, conv0_d, conv1_d, u_d, vt_d, w3_d, out_d):
    with ExitStack() as ctx:
        def sb(name, shape, dt=F32):
            return ctx.enter_context(nc.sbuf_tensor(name, shape, dt))

        def psum(name):
            return ctx.enter_context(nc.psum_tensor(name, [P, 512], F32))

        def sem(name):
            return ctx.enter_context(nc.semaphore(name))

        ps_t = [psum("ps_t0"), psum("ps_t1")]
        ps_sc = psum("ps_sc")
        ps_x = psum("ps_x")
        ps_a = psum("ps_a")
        ps_b = psum("ps_b")
        ps_c = psum("ps_c")
        ps_o = psum("ps_o")

        ints = sb("ints", [P, 3, EC], I32)
        smalls = sb("smalls", [P, SMALLS])
        biases = sb("biases", [P, D])
        ev = sb("ev", [2, D])
        x0 = sb("x0", [P, D])
        wkq = sb("wkq", [P, DC, D])
        wv = sb("wv", [P, DC, D])
        conv_w = [[sb(f"conv{l}_w{b}", [P, DC, D]) for b in range(BASES + 1)] for l in range(2)]
        u_w = sb("u_w", [P, DC, RANK])
        vt_w = sb("vt_w", [RANK, D])
        w3 = sb("w3", [P, DC, D])
        iota = sb("iota", [P, RELS * P])
        ident = sb("ident", [P, P])
        ones = sb("ones", [P, P])
        eq_b = sb("eq_b", [P, 2, 2, P])

        ends = sb("ends", [P, 3, EC])
        norm_hl = sb("norm_hl", [P, 2, EC], F32R)
        gate = sb("gate", [P, 4, EC])
        gate_hl = sb("gate_hl", [P, 2, EC], F32R)
        src_oh = sb("src_oh", [P, RING, P], F32R)
        dst_oh = sb("dst_oh", [P, RING, 3, P], F32R)
        src_n = sb("src_n", [P, RING, 2, P], F32R)
        key_oh = sb("key_oh", [P, RING, RELS * P], F32R)

        cnt_s = sb("cnt_s", [P, 2, P])
        gate_c = sb("gate_c", [P, P])
        t_sb = sb("t_sb", [P, RELS, P])
        adj_w = [sb(f"adj_w{l}", [P, BASES, P]) for l in range(2)]
        adj_sum = sb("adj_sum", [P, P])
        adj_t = sb("adj_t", [P, P])
        cnt_i = sb("cnt_i", [P, P])
        norm_row = sb("norm_row", [P, P])
        norm_t = sb("norm_t", [P, P])
        norm_adj = sb("norm_adj", [P, P])
        deg = sb("deg", [P, 3])

        stats = sb("stats", [P, 8])
        std = sb("std", [P, 4])
        rstd = sb("rstd", [P, 4])
        tot = sb("tot", [P, 4])
        neg_mean = sb("neg_mean", [P, 4])
        ssq = sb("ssq", [P, 4])
        squares = sb("squares", [P, D])
        h0 = sb("h0", [P, D])
        h_t = sb("h_t", [P, DC, P])
        kq = sb("kq", [P, D])
        kq_t = sb("kq_t", [P, 4, P])
        v_sb = sb("v_sb", [P, D])
        bias_s = sb("bias_s", [P, 2, P])
        att = sb("att", [P, 2, P])
        row_max = sb("row_max", [P, 2])
        prob = sb("prob", [P, P])
        prob_s = sb("prob_s", [P, 2, P])
        row_sum = sb("row_sum", [P, 2])
        gate_mass = sb("gate_mass", [P, 2])
        prob_t = sb("prob_t", [P, P])
        mass_t = sb("mass_t", [2, P])
        x1 = sb("x1", [P, D])
        x2 = sb("x2", [P, D])
        x3 = sb("x3", [P, D])
        x4 = sb("x4", [P, D])
        cen = sb("cen", [P, D])
        hb = sb("hb", [P, BASES, D])
        loop_sb = sb("loop_sb", [P, D])
        h1 = sb("h1", [P, D])
        scaled = sb("scaled", [P, 2, P])
        z_t = sb("z_t", [P, DC, P])
        low = sb("low", [RANK, P])
        bias3_b = sb("bias3_b", [P, D])

        names = """ld_ints ld_smalls ld_x ld_biases ld_ev ld_wkq ld_wv ld_u ld_vt ld_w3
            iota_ready ident_ready ones_ready var0 std0 h0_ready h0_turned h_t0 ends_ready gate_z gate_e sc_rows
             sc_used sc_taken t_rows t_used t_taken kq_done kq_taken v_done v_taken kq_turned kq_t_ready
            eq_ready qk_done att_max prob_ready mass_ready p_turned p_t_ready m_done x1_ready
            mean_ready ssq_ready std_ready cen_ready g_turned g_t_ready hb_done hb_taken loop_done loop_taken
            adj0_ready adj1_ready agg_done h1_ready h1_turned h1_t_ready conv_done x2_ready
            adj_sum_ready adj_turned adj_t_ready deg_ready deg_std norm_row_ready norm_turned norm_t_ready
            norm_turned2 norm_ready bias3_done bias3_ready scaled_ready z_done z_taken low_done low_taken l2_done
            x3_ready l3_done x4_ready stored chain_v chain_a chain_g""".split()
        S = {n: sem(n) for n in names}
        ld_conv = [[sem(f"ld_conv{l}_{b}") for b in range(BASES + 1)] for l in range(2)]

        block = ctx.enter_context(nc.Block())

        @block.sync
        def _(sp):
            sp.dma_start(x0[:], x_d).then_inc(S["ld_x"], 16)
            sp.dma_start(ints[:], ints_d).then_inc(S["ld_ints"], 16)
            sp.dma_start(smalls[:], smalls_d).then_inc(S["ld_smalls"], 16)
            sp.dma_start(wkq[:], wkq_d.rearrange("(c p) n -> p c n", p=P)).then_inc(S["ld_wkq"], 16)
            sp.dma_start(wv[:], wv_d.rearrange("(c p) n -> p c n", p=P)).then_inc(S["ld_wv"], 16)
            for j in range(4):
                sp.dma_start(biases[32 * j:32 * j + 1, :], biases_d[j:j + 1, :]).then_inc(S["ld_biases"], 16)
            sp.dma_start(ev[:], ev_d).then_inc(S["ld_ev"], 16)
            for l, w_d in enumerate((conv0_d, conv1_d)):
                for b in range(BASES + 1):
                    sp.dma_start(conv_w[l][b][:], w_d[b].rearrange("(c p) n -> p c n", p=P)).then_inc(ld_conv[l][b], 16)
            sp.dma_start(u_w[:], u_d.rearrange("(c p) n -> p c n", p=P)).then_inc(S["ld_u"], 16)
            sp.dma_start(vt_w[:], vt_d).then_inc(S["ld_vt"], 16)
            sp.dma_start(w3[:], w3_d.rearrange("(c p) n -> p c n", p=P)).then_inc(S["ld_w3"], 16)
            sp.wait_ge(S["x4_ready"], 1)
            sp.dma_start(out_d, x4[:]).then_inc(S["stored"], 16)
            sp.wait_ge(S["stored"], 16)

        @block.gpsimd
        def _(pool):
            chain = [0]

            def link(ins):
                chain[0] += 1
                ins.then_inc(S["chain_g"], 1)
                pool.wait_ge(S["chain_g"], chain[0])

            link(pool.memset(ident[:], 0.0))
            pool.affine_select(out=ident[:], in_=ident[:], compare_op=ALU.not_equal, fill=1.0, base=0,
                               pattern=[[-1, P]], channel_multiplier=1).then_inc(S["ident_ready"], 1)
            pool.iota(iota[:], pattern=[[1, RELS * P]], base=0, channel_multiplier=0,
                      allow_small_or_imprecise_dtypes=True).then_inc(S["iota_ready"], 1)
            pool.memset(ones[:], 1.0).then_inc(S["ones_ready"], 1)

        @block.scalar
        def _(act):
            act.wait_ge(S["var0"], 1)
            act.activation(std[:, 0:1], stats[:, 7:8], ACT.Sqrt, bias=0.0, scale=1.0).then_inc(S["std0"], 1)
            act.wait_ge(S["h0_turned"], 1)
            act.activation(h_t[:].rearrange("p c n -> p (c n)"), ps_x[:], ACT.Relu).then_inc(S["h_t0"], 1)
            act.wait_ge(S["gate_z"], 1)
            act.activation(gate[:, 1, :], gate[:, 0, :], ACT.Exp, scale=-1.0).then_inc(S["gate_e"], 1)
            act.wait_ge(S["kq_done"], 1)
            act.copy(kq[:], ps_a[:]).then_inc(S["kq_taken"], 1)
            act.wait_ge(S["v_done"], 1)
            act.copy(v_sb[:], ps_b[:]).then_inc(S["v_taken"], 1)
            act.wait_ge(S["kq_turned"], 1)
            act.copy(kq_t[:].rearrange("p c n -> p (c n)"), ps_x[:]).then_inc(S["kq_t_ready"], 1)
            act.wait_ge(S["att_max"], 1)
            act.activation(prob[:], att[:, 1, :], ACT.Exp, bias=row_max[:, 1:2], scale=SCALE,
                           accum_out=row_sum[:, 0:1]).then_inc(S["prob_ready"], 1)
            act.wait_ge(S["p_turned"], 1)
            act.copy(prob_t[:], ps_x[:, 0:P]).then_inc(S["p_t_ready"], 1)
            act.copy(mass_t[:], ps_x[0:2, P:2 * P]).then_inc(S["p_t_ready"], 1)
            act.wait_ge(S["t_used"], EC)
            for i in range(2):
                act.copy(t_sb[:, 4 * i:4 * i + 4, :].rearrange("p r n -> p (r n)"), ps_t[i][:]).then_inc(S["t_taken"], 1)

            def deviation(n, x):
                act.wait_ge(S["mean_ready"], n)
                if n > 1:
                    act.wait_ge(S["std_ready"], n - 1)
                act.activation(squares[:], x[:], ACT.Square, bias=neg_mean[:, n:n + 1],
                               accum_out=ssq[:, n:n + 1]).then_inc(S["ssq_ready"], 1)
                act.wait_ge(S["ssq_ready"], 2 * n)
                act.activation(std[:, n:n + 1], ssq[:, n:n + 1], ACT.Sqrt).then_inc(S["std_ready"], 1)

            deviation(1, x1)
            act.wait_ge(S["deg_ready"], 1)
            act.activation(deg[:, 1:2], deg[:, 0:1], ACT.Sqrt).then_inc(S["deg_std"], 1)
            act.wait_ge(S["g_turned"], 1)
            act.activation(h_t[:].rearrange("p c n -> p (c n)"), ps_x[:], ACT.Relu).then_inc(S["g_t_ready"], 1)
            act.wait_ge(S["mean_ready"], 1)
            for b in range(BASES):
                act.wait_ge(S["hb_done"], b + 1)
                if b == 0:
                    act.wait_ge(S["x1_ready"], 2)
                act.activation(hb[:, b, :], (ps_a, ps_b)[b % 2][:], ACT.Copy, scale=rstd[:, 1:2]).then_inc(S["hb_taken"], 1)
            act.wait_ge(S["loop_done"], 1)
            act.activation(loop_sb[:], ps_c[:], ACT.Copy, scale=rstd[:, 1:2]).then_inc(S["loop_taken"], 1)
            act.wait_ge(S["h1_turned"], 1)
            act.activation(h_t[:].rearrange("p c n -> p (c n)"), ps_x[:], ACT.Relu).then_inc(S["h1_t_ready"], 1)
            for b in range(BASES):
                act.wait_ge(S["hb_done"], BASES + b + 1)
                act.copy(hb[:, b, :], (ps_a, ps_b)[b % 2][:]).then_inc(S["hb_taken"], 1)
            deviation(2, x2)
            act.wait_ge(S["z_done"], 1)
            act.copy(z_t[:].rearrange("p c n -> p (c n)"), ps_x[:]).then_inc(S["z_taken"], 1)
            act.wait_ge(S["low_done"], 1)
            act.activation(low[:], ps_a[0:RANK, 0:P], ACT.Copy, scale=smalls[0:RANK, S2:S2 + 1]).then_inc(S["low_taken"], 1)
            deviation(3, x3)
            act.wait_ge(S["z_done"], 2)
            act.copy(z_t[:].rearrange("p c n -> p (c n)"), ps_x[:]).then_inc(S["z_taken"], 1)

        @block.vector
        def _(dve):
            chain = [0]

            def link(ins):
                chain[0] += 1
                ins.then_inc(S["chain_v"], 1)
                dve.wait_ge(S["chain_v"], chain[0])

            dve.wait_ge(S["ld_x"], 16)
            link(dve.bn_stats(stats[:, 0:6], x0[:]))
            link(dve.bn_aggr(stats[:, 6:8], stats[:, 0:6]))
            dve.tensor_scalar(stats[:, 7:8], stats[:, 7:8], LN_EPS, None, ALU.add).then_inc(S["var0"], 1)
            dve.wait_ge(S["ld_ints"], 16)
            dve.tensor_copy(ends[:, 0:2, :], ints[:, 0:2, :])
            dve.scalar_tensor_tensor(ends[:, 2, :], ints[:, 2, :], float(P), ints[:, 1, :], ALU.mult, ALU.add)
            dve.wait_ge(S["ld_smalls"], 16)
            dve.tensor_copy(norm_hl[:, 0, :], smalls[:, NORM:NORM + EC])
            dve.tensor_scalar(gate[:, 0, :], smalls[:, W1:W1 + EC], smalls[:, IDXB:IDXB + 1], smalls[:, IDXM:IDXM + 1],
                              ALU.subtract, ALU.mult).then_inc(S["gate_z"], 1)
            for t in range(2):
                last = dve.tensor_copy(eq_b[:, :, t, :], smalls[:, EQ + t:EQ + 4:2].rearrange("p (c o) -> p c o", o=1).broadcast_to([P, 2, P]))
            last.then_inc(S["eq_ready"], 1)
            dve.wait_ge(S["std0"], 1)
            link(dve.reciprocal(rstd[:, 0:1], std[:, 0:1]))
            dve.tensor_scalar(h0[:], x0[:], stats[:, 6:7], rstd[:, 0:1], ALU.subtract, ALU.mult).then_inc(S["h0_ready"], 1)
            dve.tensor_tensor(norm_hl[:, 1, :], smalls[:, NORM:NORM + EC], norm_hl[:, 0, :].bitcast(F32), ALU.subtract)
            dve.wait_ge(S["gate_e"], 1)
            link(dve.tensor_scalar(gate[:, 2, :], gate[:, 1, :], 3e38, 1.0, ALU.min, ALU.add))
            link(dve.reciprocal(gate[:, 3, :], gate[:, 2, :]))
            link(dve.tensor_copy(gate_hl[:, 0, :], gate[:, 3, :]))
            link(dve.tensor_tensor(gate_hl[:, 1, :], gate[:, 3, :], gate_hl[:, 0, :].bitcast(F32), ALU.subtract))
            dve.wait_ge(S["iota_ready"], 1)

            def gate_rows(c):
                r = c % RING
                if c >= RING:
                    dve.wait_ge(S["sc_used"], c - RING + 1)
                dve.tensor_scalar(src_oh[:, r, :], iota[:, 0:P], ends[:, 0, c:c + 1], None, ALU.is_equal).then_inc(S["sc_rows"], 1)
                dve.tensor_scalar(dst_oh[:, r, 0, :], iota[:, 0:P], ends[:, 1, c:c + 1], None, ALU.is_equal).then_inc(S["sc_rows"], 1)
                for j in range(2):
                    dve.tensor_scalar(dst_oh[:, r, 1 + j, :], iota[:, 0:P], ends[:, 1, c:c + 1], gate_hl[:, j, c:c + 1].bitcast(F32),
                                      ALU.is_equal, ALU.mult).then_inc(S["sc_rows"], 1)

            def type_rows(c):
                r = c % RING
                if c >= RING:
                    dve.wait_ge(S["t_used"], c - RING + 1)
                for j in range(2):
                    dve.tensor_scalar(src_n[:, r, j, :], iota[:, 0:P], ends[:, 0, c:c + 1], norm_hl[:, j, c:c + 1].bitcast(F32),
                                      ALU.is_equal, ALU.mult).then_inc(S["t_rows"], 1)
                dve.tensor_scalar(key_oh[:, r, :], iota[:], ends[:, 2, c:c + 1], None, ALU.is_equal).then_inc(S["t_rows"], 1)

            for c in range(EC):
                gate_rows(c)
            dve.wait_ge(S["sc_used"], EC)
            link(dve.tensor_copy(cnt_s[:].rearrange("p a n -> p (a n)"), ps_sc[:, 0:2 * P]))
            dve.tensor_tensor(gate_c[:], cnt_s[:, 0, :], cnt_s[:, 1, :], ALU.subtract).then_inc(S["sc_taken"], 1)
            for c in range(4):
                type_rows(c)
            dve.wait_ge(S["qk_done"], 1)
            dve.wait_ge(S["sc_taken"], 1)
            link(dve.tensor_copy(gate[:, 0, 0:2], ps_c[:, 3 * P:3 * P + 2]))
            dve.scalar_tensor_tensor(bias_s[:, 0, :], ps_c[:, P:2 * P], gate[:, 0, 0:1], cnt_s[:, 1, :], ALU.add, ALU.mult)
            link(dve.scalar_tensor_tensor(bias_s[:, 1, :], ps_c[:, 2 * P:3 * P], gate[:, 0, 1:2], gate_c[:], ALU.add, ALU.mult))
            link(dve.scalar_tensor_tensor(att[:, 0, :], ps_c[:, 0:P], 2.0, bias_s[:, 0, :], ALU.mult, ALU.add))
            link(dve.tensor_tensor(att[:, 1, :], att[:, 0, :], bias_s[:, 1, :], ALU.add))
            link(dve.reduce_max(row_max[:, 0:1], att[:, 1, :], AX_X))
            dve.tensor_scalar(row_max[:, 1:2], row_max[:, 0:1], -SCALE, None, ALU.mult).then_inc(S["att_max"], 1)
            dve.wait_ge(S["prob_ready"], 1)
            dve.tensor_tensor_reduce(out=prob_s[:, 0, :], in0=prob[:], in1=cnt_s[:, 1, :], scale=1.0, scalar=0.0,
                                     op0=ALU.mult, op1=ALU.add, accum_out=gate_mass[:, 0:1]).then_inc(S["mass_ready"], 1)
            dve.tensor_tensor_reduce(out=prob_s[:, 1, :], in0=prob[:], in1=gate_c[:], scale=1.0, scalar=0.0,
                                     op0=ALU.mult, op1=ALU.add, accum_out=gate_mass[:, 1:2]).then_inc(S["mass_ready"], 1)
            link(dve.reciprocal(row_sum[:, 1:2], row_sum[:, 0:1]))
            for c in range(4, EC):
                type_rows(c)
            dve.wait_ge(S["m_done"], 1)
            dve.scalar_tensor_tensor(x1[:], ps_o[:], row_sum[:, 1:2], x0[:], ALU.mult, ALU.add,
                                     accum_out=tot[:, 1:2]).then_inc(S["x1_ready"], 1)

            def center(n, x, relu):
                dve.tensor_scalar(neg_mean[:, n:n + 1], tot[:, n:n + 1], -1.0 / D, None, ALU.mult).then_inc(S["mean_ready"], 1)
                dve.wait_ge(S["mean_ready"], n)
                dve.tensor_scalar(cen[:], x[:], neg_mean[:, n:n + 1], 0.0 if relu else None, ALU.add,
                                  ALU.max if relu else ALU.bypass).then_inc(S["cen_ready"], 1)

            def inverse(n):
                dve.wait_ge(S["ssq_ready"], n)

            dve.wait_ge(S["x1_ready"], 1)
            center(1, x1, False)

            def rstd_of(n):
                dve.wait_ge(S["ssq_ready"], 2 * n - 1)
                dve.tensor_scalar(ssq[:, n:n + 1], ssq[:, n:n + 1], 1.0 / D, LN_EPS, ALU.mult, ALU.add).then_inc(S["ssq_ready"], 1)
                dve.wait_ge(S["std_ready"], n)
                dve.reciprocal(rstd[:, n:n + 1], std[:, n:n + 1]).then_inc(S["x1_ready"], 1)

            rstd_of(1)
            dve.wait_ge(S["t_taken"], 2)

            def mix(l):
                comp = COMP0 if l == 0 else COMP1
                for r in range(RELS):
                    for b in range(BASES):
                        k = comp + r * BASES + b
                        if r == 0:
                            ins = dve.tensor_scalar(adj_w[l][:, b, :], t_sb[:, r, :], smalls[:, k:k + 1], None, ALU.mult)
                        else:
                            ins = dve.scalar_tensor_tensor(adj_w[l][:, b, :], t_sb[:, r, :], smalls[:, k:k + 1],
                                                           adj_w[l][:, b, :], ALU.mult, ALU.add)
                        ins.then_inc(S["adj0_ready" if l == 0 else "adj1_ready"], 1)
                    if r < RELS - 1:
                        dve.wait_ge(S["adj0_ready" if l == 0 else "adj1_ready"], BASES * (r + 1))

            mix(0)
            link(dve.scalar_tensor_tensor(cnt_i[:], cnt_s[:, 0, :], 1.0, ident[:], ALU.mult, ALU.add, accum_out=deg[:, 0:1]))
            dve.tensor_scalar(deg[:, 0:1], deg[:, 0:1], 1.0, None, ALU.mult).then_inc(S["deg_ready"], 1)
            mix(1)
            dve.tensor_reduce(adj_sum[:], t_sb[:].rearrange("p r n -> p n r"), AX_X, ALU.add).then_inc(S["adj_sum_ready"], 1)
            dve.wait_ge(S["deg_std"], 1)
            link(dve.reciprocal(deg[:, 2:3], deg[:, 1:2]))
            dve.tensor_scalar(norm_row[:], cnt_i[:], deg[:, 2:3], None, ALU.mult).then_inc(S["norm_row_ready"], 1)
            dve.wait_ge(S["adj_turned"], 1)
            dve.tensor_copy(adj_t[:], ps_sc[:, 0:P]).then_inc(S["adj_t_ready"], 1)
            dve.wait_ge(S["norm_turned"], 1)
            dve.tensor_scalar(norm_t[:], ps_sc[:, P:2 * P], deg[:, 2:3], None, ALU.mult).then_inc(S["norm_t_ready"], 1)
            dve.wait_ge(S["norm_turned2"], 1)
            dve.tensor_copy(norm_adj[:], ps_sc[:, 2 * P:3 * P]).then_inc(S["norm_ready"], 1)
            dve.wait_ge(S["bias3_done"], 1)
            dve.tensor_copy(bias3_b[:], ps_t[0][:]).then_inc(S["bias3_ready"], 1)
            dve.wait_ge(S["agg_done"], 1)
            dve.wait_ge(S["loop_taken"], 1)
            dve.tensor_tensor(h1[:], ps_o[:], loop_sb[:], ALU.add).then_inc(S["h1_ready"], 1)
            dve.wait_ge(S["conv_done"], 1)
            dve.scalar_tensor_tensor(x2[:], ps_o[:], 1.0, x1[:], ALU.mult, ALU.add, accum_out=tot[:, 2:3]).then_inc(S["x2_ready"], 1)
            dve.wait_ge(S["x2_ready"], 1)
            dve.wait_ge(S["g_turned"], 1)
            center(2, x2, True)
            rstd_of(2)
            dve.wait_ge(S["x1_ready"], 3)
            dve.wait_ge(S["adj_t_ready"], 1)
            dve.tensor_scalar(scaled[:, 0, :], adj_t[:], rstd[:, 2:3], None, ALU.mult).then_inc(S["scaled_ready"], 1)
            dve.wait_ge(S["l2_done"], 1)
            dve.scalar_tensor_tensor(x3[:], ps_b[:], 0.0, x2[:], ALU.max, ALU.add, accum_out=tot[:, 3:4]).then_inc(S["x3_ready"], 1)
            dve.wait_ge(S["x3_ready"], 1)
            center(3, x3, True)
            rstd_of(3)
            dve.wait_ge(S["x1_ready"], 4)
            dve.wait_ge(S["norm_ready"], 1)
            dve.tensor_scalar(scaled[:, 1, :], norm_adj[:], rstd[:, 3:4], None, ALU.mult).then_inc(S["scaled_ready"], 1)
            dve.wait_ge(S["l3_done"], 1)
            dve.scalar_tensor_tensor(x4[:], ps_c[:], 0.0, x3[:], ALU.max, ALU.add).then_inc(S["x4_ready"], 1)

        @block.tensor
        def _(pe):
            def dense(out, acts, w, start=True, stop=True):
                for c in range(DC):
                    last = pe.matmul(out, acts[:, c, :], w[:, c, :], start=start and c == 0, stop=stop and c == DC - 1)
                return last

            def turn(src):
                for c in range(DC):
                    last = pe.transpose(ps_x[:, c * P:(c + 1) * P], src[:, c * P:(c + 1) * P], ident[:])
                return last

            def type_sums(c):
                r = c % RING
                pe.wait_ge(S["t_rows"], 3 * (c + 1))
                for j in range(2):
                    for i in range(2):
                        last = pe.matmul(ps_t[i][:], src_n[:, r, j, :], key_oh[:, r, i * 512:(i + 1) * 512],
                                         start=(c == 0 and j == 0), stop=(c == EC - 1 and j == 1))
                last.then_inc(S["t_used"], 1)

            pe.wait_ge(S["ident_ready"], 1)
            pe.wait_ge(S["h0_ready"], 1)
            turn(h0).then_inc(S["h0_turned"], 1)
            for c in range(EC):
                r = c % RING
                pe.wait_ge(S["sc_rows"], 4 * (c + 1))
                def both(stop):
                    return pe.matmul(ps_sc[:, 0:2 * P], src_oh[:, r, :], dst_oh[:, r, 0:2, :].rearrange("p a n -> p (a n)"),
                                     start=(c == 0), stop=stop)

                if c < EC - 1:
                    both(False)
                last = pe.matmul(ps_sc[:, P:2 * P], src_oh[:, r, :], dst_oh[:, r, 2, :], start=False, stop=False)
                if c == EC - 1:
                    last = both(True)
                last.then_inc(S["sc_used"], 1)
            pe.wait_ge(S["h_t0"], 1)
            pe.wait_ge(S["ld_wkq"], 16)
            dense(ps_a[:], h_t, wkq).then_inc(S["kq_done"], 1)
            pe.wait_ge(S["ld_wv"], 16)
            dense(ps_b[:], h_t, wv).then_inc(S["v_done"], 1)
            pe.wait_ge(S["kq_taken"], 1)
            turn(kq).then_inc(S["kq_turned"], 1)
            for c in range(2):
                type_sums(c)
            pe.wait_ge(S["kq_t_ready"], 1)
            pe.wait_ge(S["eq_ready"], 1)
            pe.wait_ge(S["ld_smalls"], 16)
            for c in range(2):
                pe.matmul(ps_c[:, 0:P], kq_t[:, 2 + c, :], kq_t[:, c, :], start=(c == 0), stop=(c == 1))
            for t in range(2):
                for c in range(2):
                    pe.matmul(ps_c[:, (1 + t) * P:(2 + t) * P], eq_b[:, c, t, :], kq_t[:, c, :], start=(c == 0), stop=(c == 1))
            for c in range(2):
                last = pe.matmul(ps_c[:, 3 * P:3 * P + 2], kq_t[:, 2 + c, :], smalls[:, EK + 2 * c:EK + 2 * c + 2],
                                 start=(c == 0), stop=(c == 1))
            last.then_inc(S["qk_done"], 1)
            for c in range(2, 4):
                type_sums(c)
            pe.wait_ge(S["prob_ready"], 1)
            pe.transpose(ps_x[:, 0:P], prob[:], ident[:])
            pe.wait_ge(S["mass_ready"], 2)
            pe.transpose(ps_x[0:2, P:2 * P], gate_mass[:], ident[:]).then_inc(S["p_turned"], 1)
            pe.wait_ge(S["p_t_ready"], 2)
            pe.wait_ge(S["v_taken"], 1)
            pe.wait_ge(S["ld_ev"], 16)
            pe.matmul(ps_o[:], prob_t[:], v_sb[:], start=True, stop=False)
            pe.matmul(ps_o[:], mass_t[:], ev[:], start=False, stop=True).then_inc(S["m_done"], 1)
            for c in range(4, EC):
                type_sums(c)
            pe.wait_ge(S["cen_ready"], 1)
            turn(cen).then_inc(S["g_turned"], 1)
            pe.wait_ge(S["g_t_ready"], 1)
            for b in range(BASES):
                if b >= 2:
                    pe.wait_ge(S["hb_taken"], b - 1)
                pe.wait_ge(ld_conv[0][b], 16)
                dense((ps_a, ps_b)[b % 2][:], h_t, conv_w[0][b]).then_inc(S["hb_done"], 1)
            pe.wait_ge(ld_conv[0][BASES], 16)
            dense(ps_c[:], h_t, conv_w[0][BASES]).then_inc(S["loop_done"], 1)
            pe.wait_ge(S["ld_biases"], 64)
            pe.wait_ge(S["ones_ready"], 1)

            def bias_row(out, j, start, stop):
                return pe.matmul(out, ones[32 * j:32 * j + 1, :], biases[32 * j:32 * j + 1, :], start=start, stop=stop)

            pe.wait_ge(S["adj0_ready"], BASES * RELS)
            bias_row(ps_o[:], 0, True, False)
            for b in range(BASES):
                pe.wait_ge(S["hb_taken"], b + 1)
                last = pe.matmul(ps_o[:], adj_w[0][:, b, :], hb[:, b, :], start=False, stop=(b == BASES - 1))
            last.then_inc(S["agg_done"], 1)
            pe.wait_ge(S["adj_sum_ready"], 1)
            pe.transpose(ps_sc[:, 0:P], adj_sum[:], ident[:]).then_inc(S["adj_turned"], 1)
            pe.wait_ge(S["norm_row_ready"], 1)
            pe.wait_ge(S["adj_t_ready"], 1)
            pe.transpose(ps_sc[:, P:2 * P], norm_row[:], ident[:]).then_inc(S["norm_turned"], 1)
            pe.wait_ge(S["norm_t_ready"], 1)
            pe.transpose(ps_sc[:, 2 * P:3 * P], norm_t[:], ident[:]).then_inc(S["norm_turned2"], 1)
            pe.wait_ge(S["t_taken"], 2)
            bias_row(ps_t[0][:], 3, True, True).then_inc(S["bias3_done"], 1)
            pe.wait_ge(S["h1_ready"], 1)
            turn(h1).then_inc(S["h1_turned"], 1)
            pe.wait_ge(S["h1_t_ready"], 1)
            bias_row(ps_o[:], 1, True, False)
            pe.wait_ge(ld_conv[1][BASES], 16)
            dense(ps_o[:], h_t, conv_w[1][BASES], start=False, stop=False)
            for b in range(BASES):
                pe.wait_ge(S["hb_taken"], BASES + b - 1)
                pe.wait_ge(ld_conv[1][b], 16)
                dense((ps_a, ps_b)[b % 2][:], h_t, conv_w[1][b]).then_inc(S["hb_done"], 1)
            pe.wait_ge(S["adj1_ready"], BASES * RELS)
            for b in range(BASES):
                pe.wait_ge(S["hb_taken"], BASES + b + 1)
                last = pe.matmul(ps_o[:], adj_w[1][:, b, :], hb[:, b, :], start=False, stop=(b == BASES - 1))
            last.then_inc(S["conv_done"], 1)

            def gather(n):
                pe.wait_ge(S["cen_ready"], n)
                pe.wait_ge(S["scaled_ready"], n - 1)
                for c in range(DC):
                    last = pe.matmul(ps_x[:, c * P:(c + 1) * P], cen[:, c * P:(c + 1) * P], scaled[:, n - 2, :], start=True, stop=True)
                last.then_inc(S["z_done"], 1)
                pe.wait_ge(S["z_taken"], n - 1)

            gather(2)
            pe.wait_ge(S["ld_u"], 16)
            for c in range(DC):
                last = pe.matmul(ps_a[0:RANK, 0:P], u_w[:, c, :], z_t[:, c, :], start=(c == 0), stop=(c == DC - 1))
            last.then_inc(S["low_done"], 1)
            bias_row(ps_b[:], 2, True, False)
            pe.wait_ge(S["low_taken"], 1)
            pe.wait_ge(S["ld_vt"], 16)
            pe.matmul(ps_b[:], low[:], vt_w[:], start=False, stop=True).then_inc(S["l2_done"], 1)
            pe.wait_ge(S["norm_ready"], 1)
            pe.wait_ge(S["bias3_ready"], 1)
            pe.matmul(ps_c[:], norm_adj[:], bias3_b[:], start=True, stop=False)
            gather(3)
            pe.wait_ge(S["ld_w3"], 16)
            dense(ps_c[:], z_t, w3, start=False).then_inc(S["l3_done"], 1)


def kernel(**inputs):
    import numpy as np
    import concourse.bacc as bacc
    from concourse.bass_utils import run_bass_kernel_spmd

    i = {k: np.asarray(v) for k, v in inputs.items()}

    def rows(a):
        return np.broadcast_to(a.reshape(1, -1), (P, a.size))

    def halves(a):
        return a.reshape(2, 2, P).transpose(2, 1, 0).reshape(P, 4)

    pad = np.zeros((P, 1), np.float32)
    pad[:RANK, 0] = i["L2_gnn_s"]
    arrays = {
        "x": i["x"],
        "ints": np.stack([i[k].reshape(P, EC) for k in ("src", "dst", "edge_type_8")], axis=1),
        "smalls": np.concatenate([
            i["edge_weight"].reshape(P, EC), i["edge_weight1"].reshape(P, EC), halves(i["L0_gnn_Ek"]), halves(i["L0_gnn_Eq"]),
            rows(i["L0_gnn_idx_bias"]), rows(i["L0_gnn_idx_mult"]), rows(i["L1_gnn_comp0"]), rows(i["L1_gnn_comp1"]), pad], axis=1),
        "biases": np.stack([i["L1_gnn_bias0"], i["L1_gnn_bias1"], i["L2_gnn_bias"], i["L3_gnn_b"]]),
        "ev": i["L0_gnn_Ev"],
        "wkq": np.concatenate([i["L0_gnn_Wk"], i["L0_gnn_Wq"]], axis=1),
        "wv": i["L0_gnn_Wv"],
        "conv0": np.concatenate([i["L1_gnn_basis0"], i["L1_gnn_loop0"][None]]),
        "conv1": np.concatenate([i["L1_gnn_basis1"], i["L1_gnn_loop1"][None]]),
        "u": i["L2_gnn_U"],
        "vt": i["L2_gnn_Vt"],
        "w3": i["L3_gnn_W"].T,
    }
    nc = bacc.Bacc("TRN2", target_bir_lowering=False, num_devices=1)
    args, maps = [], {}
    for name, a in arrays.items():
        a = np.ascontiguousarray(a)
        maps[f"in_{name}"] = a
        args.append(nc.dram_tensor(f"in_{name}", a.shape, mybir.dt.from_np(a.dtype), kind="ExternalInput").ap())
    args.append(nc.dram_tensor("out_0", (P, D), F32, kind="ExternalOutput").ap())
    gnn_stack(nc, *args)
    r = run_bass_kernel_spmd(nc, [maps], core_ids=[0])
    return r.results[0]["out_0"]
```

```python
from contextlib import ExitStack

import concourse.bass as bass
from concourse import mybir

ALU = mybir.AluOpType
ACT = mybir.ActivationFunctionType
AX_X = mybir.AxisListType.X
F32 = mybir.dt.float32
F32R = mybir.dt.float32r
I32 = mybir.dt.int32
BF16 = mybir.dt.bfloat16

P = 128
D = 512
DC = D // P
EC = 16
RELS = 8
BASES = 4
HID = 256
RANK = 64
LN_EPS = 1e-5
SCALE = float(D) ** -0.5
RING = 4
BATCH = 4
NB = EC // BATCH
TILES = 2 * (BASES + 1)
RAW = 5
SLOTS = 5
HALF = D // 2
WARM = 25
LO_ON_VECTOR = (3, 7)

NORM, W1, EK, EQ, IDXB, IDXM, COMP0, COMP1, S2, SMALLS = 0, 16, 32, 36, 40, 41, 42, 74, 106, 107


def gnn_stack(nc: bass.Bass, x_d, ints_d, smalls_d, biases_d, ev_d, wkq_d, wv_d, conv_d, u_d, vt_d, w3_d, out_d):
    with ExitStack() as ctx:
        def sb(name, shape, dt=F32):
            return ctx.enter_context(nc.sbuf_tensor(name, shape, dt))

        def psum(name):
            return ctx.enter_context(nc.psum_tensor(name, [P, D], F32))

        def sem(name):
            return ctx.enter_context(nc.semaphore(name))

        ps_t = [psum("ps_t0"), psum("ps_t1")]
        ps_sc = psum("ps_sc")
        ps_x = psum("ps_x")
        ps_a = psum("ps_a")
        ps_b = psum("ps_b")
        ps_c = psum("ps_c")
        ps_o = psum("ps_o")
        m_banks = (ps_o, ps_c)
        turned_banks = ((ps_x, ps_o), (ps_x, ps_t[1]))
        agg_banks = (ps_o, ps_t[0])
        z_banks = (ps_x, ps_t[1])
        l2_banks = (ps_b, ps_t[0])
        l3_banks = (ps_c, ps_o)

        raw = [sb(f"raw{i}", [P, DC, D]) for i in range(RAW)]
        slot = [sb(f"slot{i}", [P, 2, DC, D], F32R) for i in range(SLOTS)]
        u_w = sb("u_w", [P, DC, RANK])
        vt_w = sb("vt_w", [RANK, D])
        bias_b = sb("bias_b", [P, 3, D])
        bias2 = sb("bias2", [1, D])
        ev = sb("ev", [2, D])
        wkq, wv, w3 = raw[0], raw[1], raw[(2 + TILES) % RAW]

        ints = sb("ints", [P, 3, EC], I32)
        smalls = sb("smalls", [P, SMALLS])
        iota = sb("iota", [P, RELS * P])
        ident = sb("ident", [P, P])
        zeros = sb("zeros", [P, HALF], BF16)
        ones = sb("ones", [1, P])
        eq_b = sb("eq_b", [P, 2, 2, P])
        ends = sb("ends", [P, 3, EC])
        norm_hl = sb("norm_hl", [P, 2, EC], F32R)
        gate = sb("gate", [P, 4, EC])
        gate_hl = sb("gate_hl", [P, 2, EC], F32R)
        hb_flat = sb("hb_flat", [P, 2 * BASES * D], F32R)
        src_oh = hb_flat[:, 0:EC * P].rearrange("p (c n) -> p c n", c=EC)
        src_n01 = hb_flat[:, EC * P:2 * EC * P].rearrange("p (k j b n) -> p k j b n", k=2, j=2, b=BATCH)
        src_n2 = sb("src_n2", [P, 2, BATCH, P], F32R)
        src_n = [src_n01[:, 0, :, :, :], src_n01[:, 1, :, :, :], src_n2[:]]
        hb_hl = hb_flat[:].rearrange("p (j b n) -> p j b n", j=2, b=BASES)
        dst_oh = slot[3][:].rearrange("p a c n -> p a (c n)").rearrange("p a (c n) -> p a c n", c=EC)
        dst_lo = slot[2][:, 0, :, :].rearrange("p c n -> p (c n)").rearrange("p (c n) -> p c n", c=EC)
        key_oh = slot[4][:].rearrange("p a c n -> p (a c n)").rearrange("p (r n) -> p r n", r=RING)

        cnt_s = sb("cnt_s", [P, 2, P])
        gate_c = sb("gate_c", [P, P])
        t_sb = sb("t_sb", [P, RELS, P])
        adj = sb("adj", [P, BASES, P])
        adj_hl = [sb(f"adj_hl{l}", [P, 2, BASES, P], F32R) for l in range(2)]
        adj_sum = sb("adj_sum", [P, P])
        adj_t = sb("adj_t", [P, P])
        cnt_i = sb("cnt_i", [P, P])
        norm_adj = sb("norm_adj", [P, P])
        deg = sb("deg", [P, 3])

        x0 = sb("x0", [P, D])
        stats = sb("stats", [P, 8])
        table = sb("table", [P, 2])
        std = sb("std", [P, 4])
        rstd = sb("rstd", [P, 4])
        tot = sb("tot", [P, 4, 2])
        neg_mean = sb("neg_mean", [P, 4])
        ssq = sb("ssq", [P, 4, 2])
        cen = sb("cen", [P, D])
        h_t = sb("h_t", [P, DC, P])
        h_hl = sb("h_hl", [P, 2, DC, P], F32R)
        kq = sb("kq", [P, D])
        kq_t = sb("kq_t", [P, 4, P])
        v_sb = sb("v_sb", [P, D])
        bias_s = sb("bias_s", [P, 2, P])
        att = sb("att", [P, 2, P])
        row_max = sb("row_max", [P, 2])
        prob = sb("prob", [P, P])
        prob_s = sb("prob_s", [P, 2, P])
        row_sum = sb("row_sum", [P, 2])
        gate_mass = sb("gate_mass", [P, 2])
        prob_t = sb("prob_t", [P, P])
        mass_t = sb("mass_t", [2, P])
        x1 = sb("x1", [P, D])
        x1_bias = sb("x1_bias", [P, D])
        x2 = sb("x2", [P, D])
        low = sb("low", [RANK, P])
        scaled, norm_row, norm_t = att, bias_s[:, 0, :], bias_s[:, 1, :]
        h0, h1, squares, loop_sb, x3, x4, z_t = x1, kq, v_sb, v_sb, kq, v_sb, h_t

        names = """ld_ints ld_smalls ld_x ld_bias_b ld_bias2 ld_ev ld_wkq ld_wv ld_u ld_vt ld_w3
            iota_ready ident_ready ones_ready var0 std0 table_ready h0_ready h0_turned h_t0 ends_ready norm_hl_ready gate_z gate_e gate_steps
            gate_hl_ready src_rows dst_rows gate_hi_rows gate_lo_rows warm_ready sc_used sc_taken src_n_rows key_rows t_used t_taken
            kq_done kq_taken v_done v_taken kq_turned kq_t_ready
            eq_ready qk_done att_max prob_ready mass_ready p_turned p_t_ready m_done x_ready x1_bias_ready
            mean_ready ssq_ready var_ready std_ready rstd_ready cen_ready turned h_hi h_lo hb_hi hb_lo
            loop_taken adj_mix adj_hi adj_lo agg_done h1_ready conv_done
            adj_sum_ready adj_turned adj_t_ready deg_ready deg_std norm_row_ready norm_t_ready
            norm_turned2 norm_ready scaled_ready z_done z_taken low_done low_taken l2_done
            l3_done x4_ready stored w_used chain_v chain_a chain_g""".split()
        S = {n: sem(n) for n in names}
        ld_tile = [sem(f"ld_tile{k}") for k in range(TILES)]
        hi_ready = sem("hi_ready")
        lo_by_vector = sem("lo_by_vector")
        lo_by_pool = sem("lo_by_pool")

        def lo_wait(eng, k):
            mine = [j for j in range(k + 1) if (j in LO_ON_VECTOR) == (k in LO_ON_VECTOR)]
            eng.wait_ge(lo_by_vector if k in LO_ON_VECTOR else lo_by_pool, len(mine))

        def raw_of(k):
            return raw[(2 + k) % RAW]

        block = ctx.enter_context(nc.Block())

        @block.sync
        def _(sp):
            sp.dma_start(ints[:], ints_d).then_inc(S["ld_ints"], 16)
            sp.dma_start(smalls[:], smalls_d).then_inc(S["ld_smalls"], 16)
            sp.dma_start(x0[:], x_d).then_inc(S["ld_x"], 16)
            sp.dma_start(wkq[:], wkq_d.rearrange("(c p) n -> p c n", p=P)).then_inc(S["ld_wkq"], 16)
            sp.dma_start(wv[:], wv_d.rearrange("(c p) n -> p c n", p=P)).then_inc(S["ld_wv"], 16)
            sp.dma_start(ev[:], ev_d).then_inc(S["ld_ev"], 16)
            for k in range(TILES):
                if k == RAW - 2:
                    sp.wait_ge(S["kq_done"], 1)
                if k == RAW - 1:
                    sp.wait_ge(S["v_done"], 1)
                if k >= RAW:
                    sp.wait_ge(hi_ready, 2 * (k - RAW + 1))
                    lo_wait(sp, k - RAW)
                sp.dma_start(raw_of(k)[:], conv_d[k].rearrange("(c p) n -> p c n", p=P)).then_inc(ld_tile[k], 16)
                if k == 4:
                    for j in range(3):
                        sp.dma_start(bias_b[:, j, :], biases_d[j:j + 1, :].broadcast_to([P, D])).then_inc(S["ld_bias_b"], 16)
                    sp.dma_start(bias2[:], biases_d[3:4, :]).then_inc(S["ld_bias2"], 16)
                    sp.dma_start(u_w[:], u_d.rearrange("(c p) n -> p c n", p=P)).then_inc(S["ld_u"], 16)
                    sp.dma_start(vt_w[:], vt_d).then_inc(S["ld_vt"], 16)
            sp.wait_ge(hi_ready, 2 * (TILES - RAW + 1))
            lo_wait(sp, TILES - RAW)
            sp.dma_start(w3[:], w3_d.rearrange("(c p) n -> p c n", p=P)).then_inc(S["ld_w3"], 16)
            for i in range(2):
                sp.wait_ge(S["x4_ready"], i + 1)
                sp.dma_start(out_d[:, i * HALF:(i + 1) * HALF], x4[:, i * HALF:(i + 1) * HALF]).then_inc(S["stored"], 16)
            sp.wait_ge(S["stored"], 32)

        def slot_free(eng, k):
            if k in (2, 3):
                eng.wait_ge(S["sc_used"], EC)
            if k == 4:
                eng.wait_ge(S["t_used"], EC)
            if k >= SLOTS:
                eng.wait_ge(S["w_used"], k - SLOTS + 1)

        def low_part(eng, k, done):
            eng.wait_ge(hi_ready, 2 * (k + 1))
            slot_free(eng, k)
            eng.tensor_tensor(slot[k % SLOTS][:, 1, :, :].rearrange("p c n -> p (c n)"), raw_of(k)[:].rearrange("p c n -> p (c n)"),
                              slot[k % SLOTS][:, 0, :, :].rearrange("p c n -> p (c n)").bitcast(F32), ALU.subtract).then_inc(done, 1)

        @block.gpsimd
        def _(pool):
            pool.iota(iota[:], pattern=[[1, RELS * P]], base=0, channel_multiplier=0,
                      allow_small_or_imprecise_dtypes=True).then_inc(S["iota_ready"], 1)
            pool.memset(ident[:], 0.0).then_inc(S["chain_g"], 1)
            pool.wait_ge(S["chain_g"], 1)
            pool.affine_select(out=ident[:], in_=ident[:], compare_op=ALU.not_equal, fill=1.0, base=0,
                               pattern=[[-1, P]], channel_multiplier=1).then_inc(S["ident_ready"], 1)
            pool.memset(ones[:], 1.0).then_inc(S["ones_ready"], 1)
            for b in range(NB):
                if b == 0:
                    pool.wait_ge(S["norm_hl_ready"], 2)
                pool.wait_ge(S["src_rows"], b + 1)
                if b >= 3:
                    low_part(pool, 0, lo_by_pool)
                    low_part(pool, 1, lo_by_pool)
                    pool.wait_ge(S["t_used"], BATCH * (b - 2))
                for j in range(2):
                    w = norm_hl[:, j, b * BATCH:(b + 1) * BATCH].bitcast(F32).rearrange("p (b o) -> p b o", o=1)
                    pool.tensor_tensor(src_n[b % 3][:, j, :, :], src_oh[:, b * BATCH:(b + 1) * BATCH, :].bitcast(F32),
                                       w.broadcast_to([P, BATCH, P]), ALU.mult).then_inc(S["src_n_rows"], 1)
            for k in range(2, TILES):
                if k not in LO_ON_VECTOR:
                    low_part(pool, k, lo_by_pool)
                if k == 4:
                    pool.wait_ge(S["x_ready"], 2)
                    pool.wait_ge(S["ld_bias_b"], 48)
                    pool.tensor_tensor(x1_bias[:], x1[:], bias_b[:, 1, :], ALU.add).then_inc(S["x1_bias_ready"], 1)

        @block.scalar
        def _(act):
            act.wait_ge(S["gate_z"], 1)
            act.activation(gate[:, 1, :], gate[:, 0, :], ACT.Exp, scale=-1.0).then_inc(S["gate_e"], 1)
            act.wait_ge(S["var0"], 2)
            act.activation(std[:, 0:1], stats[:, 7:8], ACT.Sqrt).then_inc(S["std0"], 1)
            act.wait_ge(S["warm_ready"], 1)
            act.activation(table[:, 0:1], zeros[:, 0:1], ACT.Exp).then_inc(S["table_ready"], 1)

            def gate_lo(c):
                b = c // BATCH
                act.wait_ge(S["dst_rows"], b + 1)
                if c == 0:
                    act.wait_ge(S["gate_hl_ready"], 2)
                act.activation(dst_lo[:, c, :], dst_oh[:, 0, c, :].bitcast(F32), ACT.Copy,
                               scale=gate_hl[:, 1, c:c + 1].bitcast(F32)).then_inc(S["gate_lo_rows"], 1)

            for c in range(4):
                gate_lo(c)
            act.wait_ge(S["h0_turned"], 1)
            act.activation(h_t[:].rearrange("p c n -> p (c n)"), ps_x[:], ACT.Relu).then_inc(S["h_t0"], 1)
            for c in range(4, EC):
                gate_lo(c)
            act.wait_ge(S["kq_done"], 1)
            act.copy(kq[:], ps_a[:]).then_inc(S["kq_taken"], 1)

            def high_part(k, halves=(0, 1)):
                act.wait_ge(ld_tile[k], 16)
                slot_free(act, k)
                for i in halves:
                    act.copy(slot[k % SLOTS][:, 0, 2 * i:2 * i + 2, :].rearrange("p c n -> p (c n)"),
                             raw_of(k)[:, 2 * i:2 * i + 2, :].rearrange("p c n -> p (c n)")).then_inc(hi_ready, 1)

            act.wait_ge(S["kq_turned"], 1)
            act.copy(kq_t[:].rearrange("p c n -> p (c n)"), ps_x[:]).then_inc(S["kq_t_ready"], 1)
            high_part(0)
            high_part(1, [0])
            act.wait_ge(S["att_max"], 1)
            act.activation(prob[:], att[:, 1, :], ACT.Exp, bias=row_max[:, 1:2], scale=SCALE,
                           accum_out=row_sum[:, 0:1]).then_inc(S["prob_ready"], 1)
            high_part(1, [1])
            act.wait_ge(S["v_done"], 1)
            act.copy(v_sb[:], ps_b[:]).then_inc(S["v_taken"], 1)
            act.wait_ge(S["p_turned"], 1)
            act.copy(prob_t[:], ps_x[:, 0:P]).then_inc(S["p_t_ready"], 1)
            act.copy(mass_t[:], ps_x[0:2, P:2 * P]).then_inc(S["p_t_ready"], 1)
            act.activation(table[:, 1:2], zeros[:, 0:1], ACT.Sqrt).then_inc(S["table_ready"], 1)

            def deviation(n, x):
                act.wait_ge(S["mean_ready"], n)
                act.activation(squares[:], x[:], ACT.Square, bias=neg_mean[:, n:n + 1],
                               accum_out=ssq[:, n, 0:1]).then_inc(S["ssq_ready"], 1)

            def root(n):
                act.wait_ge(S["var_ready"], n)
                act.activation(std[:, n:n + 1], ssq[:, n, 1:2], ACT.Sqrt).then_inc(S["std_ready"], 1)

            def turned_high(n):
                for i in range(2):
                    act.wait_ge(S["turned"], 2 * (n - 1) + i + 1)
                    act.activation(h_hl[:, 0, 2 * i:2 * i + 2, :].rearrange("p c n -> p (c n)"), turned_banks[n - 1][i][:, 0:HALF],
                                   ACT.Relu).then_inc(S["h_hi"], 1)

            def basis_high(l, b):
                act.wait_ge(S["w_used"], (BASES + 1) * l + b + 1)
                if l == 1 and b == 0:
                    act.wait_ge(S["agg_done"], 2)
                ps = (ps_a, ps_b)[b % 2]
                if l == 0:
                    act.activation(hb_hl[:, 0, b, :], ps[:], ACT.Copy, scale=rstd[:, 1:2]).then_inc(S["hb_hi"], 1)
                else:
                    act.copy(hb_hl[:, 0, b, :], ps[:]).then_inc(S["hb_hi"], 1)

            act.wait_ge(S["m_done"], 2)
            deviation(1, x1)
            turned_high(1)
            root(1)
            act.wait_ge(S["deg_ready"], 1)
            act.activation(deg[:, 1:2], deg[:, 0:1], ACT.Sqrt).then_inc(S["deg_std"], 1)
            high_part(2)
            high_part(3)
            act.wait_ge(S["t_used"], EC)
            for i in range(2):
                act.copy(t_sb[:, 4 * i:4 * i + 4, :].rearrange("p r n -> p (r n)"), ps_t[i][:]).then_inc(S["t_taken"], 1)
            high_part(4)
            act.wait_ge(S["rstd_ready"], 1)
            basis_high(0, 0)
            high_part(5)
            basis_high(0, 1)
            high_part(6)
            basis_high(0, 2)
            high_part(7)
            basis_high(0, 3)
            act.wait_ge(S["adj_mix"], BASES * RELS)
            act.copy(adj_hl[0][:, 0, :, :].rearrange("p b n -> p (b n)"), adj[:].rearrange("p b n -> p (b n)")).then_inc(S["adj_hi"], 1)
            high_part(8)
            turned_high(2)
            high_part(9)
            basis_high(1, 0)
            basis_high(1, 1)
            basis_high(1, 2)
            act.wait_ge(S["adj_mix"], 2 * BASES * RELS)
            act.copy(adj_hl[1][:, 0, :, :].rearrange("p b n -> p (b n)"), adj[:].rearrange("p b n -> p (b n)")).then_inc(S["adj_hi"], 1)
            basis_high(1, 3)

            def take_z(n):
                for i in range(2):
                    act.wait_ge(S["z_done"], 2 * (n - 1) + i + 1)
                    act.copy(z_t[:, 2 * i:2 * i + 2, :].rearrange("p c n -> p (c n)"), z_banks[i][:, 0:HALF]).then_inc(S["z_taken"], 1)

            deviation(2, x2)
            root(2)
            take_z(1)
            act.wait_ge(S["low_done"], 1)
            act.activation(low[:], ps_a[0:RANK, 0:P], ACT.Copy, scale=smalls[0:RANK, S2:S2 + 1]).then_inc(S["low_taken"], 1)
            deviation(3, x3)
            root(3)
            take_z(2)

        @block.vector
        def _(dve):
            chain = [0]

            def link(ins):
                chain[0] += 1
                ins.then_inc(S["chain_v"], 1)
                dve.wait_ge(S["chain_v"], chain[0])

            def spread(a):
                return a.rearrange("p (b o) -> p b o", o=1).broadcast_to([P, BATCH, P])

            def batch_rows(b, part):
                cs = slice(b * BATCH, (b + 1) * BATCH)
                columns = iota[:, 0:P].rearrange("p (o n) -> p o n", o=1).broadcast_to([P, BATCH, P])
                if part == 0:
                    dve.tensor_tensor(src_oh[:, cs, :], columns, spread(ends[:, 0, cs]), ALU.is_equal).then_inc(S["src_rows"], 1)
                if part == 1:
                    dve.tensor_tensor(dst_oh[:, 0, cs, :], columns, spread(ends[:, 1, cs]), ALU.is_equal).then_inc(S["dst_rows"], 1)
                if part == 2:
                    dve.wait_ge(S["dst_rows"], b + 1)
                    dve.tensor_tensor(dst_oh[:, 1, cs, :], dst_oh[:, 0, cs, :].bitcast(F32),
                                      spread(gate_hl[:, 0, cs].bitcast(F32)), ALU.mult).then_inc(S["gate_hi_rows"], 1)

            def type_rows(c):
                if c >= RING:
                    dve.wait_ge(S["t_used"], c - RING + 1)
                dve.tensor_scalar(key_oh[:, c % RING, :], iota[:], ends[:, 2, c:c + 1], None, ALU.is_equal).then_inc(S["key_rows"], 1)

            dve.memset(zeros[:], 0.0).then_inc(S["warm_ready"], 1)
            dve.wait_ge(S["ld_ints"], 16)
            dve.tensor_copy(ends[:, 0:2, :], ints[:, 0:2, :]).then_inc(S["ends_ready"], 1)
            dve.scalar_tensor_tensor(ends[:, 2, :], ints[:, 2, :], float(P), ints[:, 1, :], ALU.mult, ALU.add).then_inc(S["ends_ready"], 1)
            dve.wait_ge(S["iota_ready"], 1)
            dve.wait_ge(S["ends_ready"], 1)
            batch_rows(0, 0)
            dve.wait_ge(S["ld_smalls"], 16)
            dve.tensor_scalar(gate[:, 0, :], smalls[:, W1:W1 + EC], smalls[:, IDXB:IDXB + 1], smalls[:, IDXM:IDXM + 1],
                              ALU.subtract, ALU.mult).then_inc(S["gate_z"], 1)
            dve.tensor_copy(norm_hl[:, 0, :], smalls[:, NORM:NORM + EC]).then_inc(S["norm_hl_ready"], 1)
            dve.wait_ge(S["ld_x"], 16)
            link(dve.bn_stats(stats[:, 0:6], x0[:]))
            dve.bn_aggr(stats[:, 6:8], stats[:, 0:6]).then_inc(S["var0"], 1)
            dve.tensor_tensor(norm_hl[:, 1, :], smalls[:, NORM:NORM + EC], norm_hl[:, 0, :].bitcast(F32),
                              ALU.subtract).then_inc(S["norm_hl_ready"], 1)
            dve.wait_ge(S["gate_e"], 1)
            dve.tensor_scalar(gate[:, 2, :], gate[:, 1, :], 3e38, 1.0, ALU.min, ALU.add).then_inc(S["gate_steps"], 1)
            dve.wait_ge(S["var0"], 1)
            dve.tensor_scalar(stats[:, 7:8], stats[:, 7:8], LN_EPS, None, ALU.add).then_inc(S["var0"], 1)
            dve.wait_ge(S["gate_steps"], 1)
            dve.reciprocal(gate[:, 3, :], gate[:, 2, :]).then_inc(S["gate_steps"], 1)
            dve.wait_ge(S["gate_steps"], 2)
            dve.tensor_copy(gate_hl[:, 0, :], gate[:, 3, :]).then_inc(S["gate_hl_ready"], 1)
            dve.wait_ge(S["std0"], 1)
            dve.reciprocal(rstd[:, 0:1], std[:, 0:1]).then_inc(S["gate_steps"], 1)
            dve.wait_ge(S["gate_hl_ready"], 1)
            dve.tensor_tensor(gate_hl[:, 1, :], gate[:, 3, :], gate_hl[:, 0, :].bitcast(F32), ALU.subtract).then_inc(S["gate_hl_ready"], 1)
            dve.wait_ge(S["gate_steps"], 3)
            dve.tensor_scalar(h0[:], x0[:], stats[:, 6:7], rstd[:, 0:1], ALU.subtract, ALU.mult).then_inc(S["h0_ready"], 1)
            batch_rows(0, 1)
            batch_rows(0, 2)
            for b in range(1, NB):
                for part in range(3):
                    batch_rows(b, part)
            for t in range(2):
                dve.tensor_copy(eq_b[:, :, t, :], smalls[:, EQ + t:EQ + 4:2].rearrange("p (c o) -> p c o", o=1)
                                .broadcast_to([P, 2, P])).then_inc(S["eq_ready"], 1)
            dve.wait_ge(S["ends_ready"], 2)
            for c in range(3):
                type_rows(c)
            dve.wait_ge(S["sc_used"], EC)
            link(dve.tensor_copy(cnt_s[:].rearrange("p a n -> p (a n)"), ps_sc[:, 0:2 * P]))
            dve.tensor_tensor(gate_c[:], cnt_s[:, 0, :], cnt_s[:, 1, :], ALU.subtract).then_inc(S["sc_taken"], 1)
            type_rows(3)
            dve.wait_ge(S["qk_done"], 1)
            dve.wait_ge(S["sc_taken"], 1)
            dve.scalar_tensor_tensor(bias_s[:, 0, :], ps_c[:, P:2 * P], ps_c[:, 3 * P:3 * P + 1], cnt_s[:, 1, :], ALU.add, ALU.mult)
            link(dve.scalar_tensor_tensor(bias_s[:, 1, :], ps_c[:, 2 * P:3 * P], ps_c[:, 3 * P + 1:3 * P + 2], gate_c[:], ALU.add, ALU.mult))
            link(dve.scalar_tensor_tensor(att[:, 0, :], ps_c[:, 0:P], 2.0, bias_s[:, 0, :], ALU.mult, ALU.add))
            link(dve.tensor_tensor_reduce(out=att[:, 1, :], in0=att[:, 0, :], in1=bias_s[:, 1, :], scale=1.0, scalar=-3e38,
                                          op0=ALU.add, op1=ALU.max, accum_out=row_max[:, 0:1]))
            dve.tensor_scalar(row_max[:, 1:2], row_max[:, 0:1], -SCALE, None, ALU.mult).then_inc(S["att_max"], 1)
            dve.wait_ge(S["prob_ready"], 1)
            dve.tensor_tensor_reduce(out=prob_s[:, 0, :], in0=prob[:], in1=cnt_s[:, 1, :], scale=1.0, scalar=0.0,
                                     op0=ALU.mult, op1=ALU.add, accum_out=gate_mass[:, 0:1]).then_inc(S["mass_ready"], 1)
            dve.tensor_tensor_reduce(out=prob_s[:, 1, :], in0=prob[:], in1=gate_c[:], scale=1.0, scalar=0.0,
                                     op0=ALU.mult, op1=ALU.add, accum_out=gate_mass[:, 1:2]).then_inc(S["mass_ready"], 1)
            link(dve.reciprocal(row_sum[:, 1:2], row_sum[:, 0:1]))

            def center(n, x, relu):
                dve.wait_ge(S["x_ready"], 2 * n)
                dve.tensor_scalar(neg_mean[:, n:n + 1], tot[:, n, 0:1], tot[:, n, 1:2], -1.0 / D, ALU.add, ALU.mult).then_inc(S["mean_ready"], 1)
                dve.wait_ge(S["mean_ready"], n)
                for i in range(2):
                    h = slice(i * HALF, (i + 1) * HALF)
                    dve.tensor_scalar(cen[:, h], x[:, h], neg_mean[:, n:n + 1], 0.0 if relu else None, ALU.add,
                                      ALU.max if relu else ALU.bypass).then_inc(S["cen_ready"], 1)

            def variance(n):
                dve.wait_ge(S["ssq_ready"], n)
                dve.tensor_scalar(ssq[:, n, 1:2], ssq[:, n, 0:1], 1.0 / D, LN_EPS, ALU.mult, ALU.add).then_inc(S["var_ready"], 1)

            def inverse(n):
                dve.wait_ge(S["std_ready"], n)
                dve.reciprocal(rstd[:, n:n + 1], std[:, n:n + 1]).then_inc(S["rstd_ready"], 1)

            def turned_low(n):
                for i in range(2):
                    dve.wait_ge(S["h_hi"], 2 * (n - 1) + i + 1)
                    dve.scalar_tensor_tensor(h_hl[:, 1, 2 * i:2 * i + 2, :].rearrange("p c n -> p (c n)"), turned_banks[n - 1][i][:, 0:HALF],
                                             0.0, h_hl[:, 0, 2 * i:2 * i + 2, :].rearrange("p c n -> p (c n)").bitcast(F32),
                                             ALU.max, ALU.subtract).then_inc(S["h_lo"], 1)

            def basis_low(l, b):
                dve.wait_ge(S["hb_hi"], BASES * l + b + 1)
                dve.wait_ge(S["rstd_ready"], 1)
                ps = (ps_a, ps_b)[b % 2]
                dve.scalar_tensor_tensor(hb_hl[:, 1, b, :], ps[:], rstd[:, 1:2] if l == 0 else 1.0, hb_hl[:, 0, b, :].bitcast(F32),
                                         ALU.mult, ALU.subtract).then_inc(S["hb_lo"], 1)

            def mix(l, rels):
                if l == 1 and 0 in rels:
                    dve.wait_ge(S["adj_hi"], 1)
                    dve.wait_ge(S["adj_lo"], 1)
                comp = (COMP0, COMP1)[l]
                for r in rels:
                    if r > 0:
                        dve.wait_ge(S["adj_mix"], BASES * (RELS * l + r))
                    for b in range(BASES):
                        k = comp + r * BASES + b
                        if r == 0:
                            ins = dve.tensor_scalar(adj[:, b, :], t_sb[:, r, :], smalls[:, k:k + 1], None, ALU.mult)
                        else:
                            ins = dve.scalar_tensor_tensor(adj[:, b, :], t_sb[:, r, :], smalls[:, k:k + 1], adj[:, b, :], ALU.mult, ALU.add)
                        ins.then_inc(S["adj_mix"], 1)

            def mix_low(l):
                dve.wait_ge(S["adj_hi"], l + 1)
                dve.tensor_tensor(adj_hl[l][:, 1, :, :].rearrange("p b n -> p (b n)"), adj[:].rearrange("p b n -> p (b n)"),
                                  adj_hl[l][:, 0, :, :].rearrange("p b n -> p (b n)").bitcast(F32), ALU.subtract).then_inc(S["adj_lo"], 1)

            for i in range(2):
                h = slice(i * HALF, (i + 1) * HALF)
                dve.wait_ge(S["m_done"], i + 1)
                dve.scalar_tensor_tensor(x1[:, h], m_banks[i][:, 0:HALF], row_sum[:, 1:2], x0[:, h], ALU.mult, ALU.add,
                                         accum_out=tot[:, 1, i:i + 1]).then_inc(S["x_ready"], 1)
            center(1, x1, False)
            type_rows(4)
            type_rows(5)
            turned_low(1)
            variance(1)
            dve.scalar_tensor_tensor(cnt_i[:], cnt_s[:, 0, :], 1.0, ident[:], ALU.mult, ALU.add, accum_out=deg[:, 0:1]).then_inc(S["deg_ready"], 1)
            type_rows(6)
            inverse(1)
            type_rows(7)
            dve.wait_ge(S["deg_std"], 1)
            link(dve.reciprocal(deg[:, 2:3], deg[:, 1:2]))
            dve.tensor_scalar(norm_row, cnt_i[:], deg[:, 2:3], None, ALU.mult).then_inc(S["norm_row_ready"], 1)
            for c in range(8, EC):
                type_rows(c)
            low_part(dve, 3, lo_by_vector)
            dve.wait_ge(S["t_taken"], 1)
            mix(0, range(0, 3))
            basis_low(0, 0)
            mix(0, [3])
            dve.wait_ge(S["t_taken"], 2)
            mix(0, [4])
            basis_low(0, 1)
            mix(0, range(5, 7))
            basis_low(0, 2)
            mix(0, [7])
            basis_low(0, 3)
            mix_low(0)
            low_part(dve, 7, lo_by_vector)
            dve.wait_ge(S["w_used"], BASES + 1)
            dve.wait_ge(S["ld_bias_b"], 48)
            dve.scalar_tensor_tensor(loop_sb[:], ps_c[:], rstd[:, 1:2], bias_b[:, 0, :], ALU.mult, ALU.add).then_inc(S["loop_taken"], 1)
            dve.wait_ge(S["loop_taken"], 1)
            for i in range(2):
                h = slice(i * HALF, (i + 1) * HALF)
                dve.wait_ge(S["agg_done"], i + 1)
                dve.tensor_tensor(h1[:, h], agg_banks[i][:, 0:HALF], loop_sb[:, h], ALU.add).then_inc(S["h1_ready"], 1)
            turned_low(2)
            mix(1, range(0, 4))
            basis_low(1, 0)
            dve.tensor_reduce(adj_sum[:], t_sb[:].rearrange("p r n -> p n r"), AX_X, ALU.add).then_inc(S["adj_sum_ready"], 1)
            mix(1, range(4, 6))
            basis_low(1, 1)
            mix(1, range(6, 8))
            basis_low(1, 2)
            basis_low(1, 3)
            mix_low(1)
            dve.wait_ge(S["adj_turned"], 1)
            dve.tensor_copy(adj_t[:], ps_sc[:, 0:P]).then_inc(S["adj_t_ready"], 1)
            dve.tensor_scalar(norm_t, ps_sc[:, P:2 * P], deg[:, 2:3], None, ALU.mult).then_inc(S["norm_t_ready"], 1)
            dve.wait_ge(S["x1_bias_ready"], 1)
            dve.wait_ge(S["w_used"], TILES)
            dve.tensor_tensor(loop_sb[:], ps_c[:], x1_bias[:], ALU.add).then_inc(S["loop_taken"], 1)
            dve.wait_ge(S["loop_taken"], 2)
            for i in range(2):
                h = slice(i * HALF, (i + 1) * HALF)
                dve.wait_ge(S["conv_done"], i + 1)
                dve.scalar_tensor_tensor(x2[:, h], agg_banks[i][:, 0:HALF], 1.0, loop_sb[:, h], ALU.mult, ALU.add,
                                         accum_out=tot[:, 2, i:i + 1]).then_inc(S["x_ready"], 1)
            center(2, x2, True)
            variance(2)
            inverse(2)
            dve.wait_ge(S["rstd_ready"], 2)
            dve.wait_ge(S["adj_t_ready"], 1)
            dve.tensor_scalar(scaled[:, 0, :], adj_t[:], rstd[:, 2:3], None, ALU.mult).then_inc(S["scaled_ready"], 1)
            dve.wait_ge(S["norm_turned2"], 1)
            dve.tensor_copy(norm_adj[:], ps_sc[:, 2 * P:3 * P]).then_inc(S["norm_ready"], 1)
            for i in range(2):
                h = slice(i * HALF, (i + 1) * HALF)
                dve.wait_ge(S["l2_done"], i + 1)
                dve.scalar_tensor_tensor(x3[:, h], l2_banks[i][:, 0:HALF], 0.0, x2[:, h], ALU.max, ALU.add,
                                         accum_out=tot[:, 3, i:i + 1]).then_inc(S["x_ready"], 1)
            center(3, x3, True)
            variance(3)
            inverse(3)
            dve.wait_ge(S["rstd_ready"], 3)
            dve.wait_ge(S["norm_ready"], 1)
            dve.tensor_scalar(scaled[:, 1, :], norm_adj[:], rstd[:, 3:4], None, ALU.mult).then_inc(S["scaled_ready"], 1)
            for i in range(2):
                h = slice(i * HALF, (i + 1) * HALF)
                dve.wait_ge(S["l3_done"], i + 1)
                dve.scalar_tensor_tensor(x4[:, h], l3_banks[i][:, 0:HALF], 0.0, x3[:, h], ALU.max, ALU.add).then_inc(S["x4_ready"], 1)

        @block.tensor
        def _(pe):
            def dense(out, acts, w, cols=slice(0, D), start=True, stop=True):
                for c in range(DC):
                    last = pe.matmul(out, acts[:, c, :], w[:, c, cols], start=start and c == 0, stop=stop and c == DC - 1)
                return last

            def turn(src, done, banks):
                n = DC // len(banks)
                for i, bank in enumerate(banks):
                    for c in range(n):
                        last = pe.transpose(bank[:, c * P:(c + 1) * P], src[:, (i * n + c) * P:(i * n + c + 1) * P], ident[:])
                    last.then_inc(done, 1)

            def type_sums(c):
                b = c // BATCH
                pe.wait_ge(S["src_n_rows"], 2 * (b + 1))
                pe.wait_ge(S["key_rows"], c + 1)
                for j in range(2):
                    for i in range(2):
                        last = pe.matmul(ps_t[i][:], src_n[b % 3][:, j, c % BATCH, :], key_oh[:, c % RING, i * 512:(i + 1) * 512],
                                         start=(c == 0 and j == 0), stop=(c == EC - 1 and j == 1))
                last.then_inc(S["t_used"], 1)

            def gate_sums(b):
                for c in range(BATCH * b, BATCH * (b + 1)):
                    s = src_oh[:, c, :]
                    d = dst_oh[:, :, c, :]
                    pe.wait_ge(S["gate_hi_rows"], b + 1)
                    if c < EC - 1:
                        pe.matmul(ps_sc[:, 0:2 * P], s, d, start=(c == 0), stop=False)
                    pe.wait_ge(S["gate_lo_rows"], c + 1)
                    last = pe.matmul(ps_sc[:, P:2 * P], s, dst_lo[:, c, :], start=False, stop=False)
                    if c == EC - 1:
                        last = pe.matmul(ps_sc[:, 0:2 * P], s, d, start=False, stop=True)
                    last.then_inc(S["sc_used"], 1)

            pe.wait_ge(S["warm_ready"], 1)
            for _ in range(WARM):
                pe.matmul(ps_o[:, 0:HALF], zeros[:, 0:P], zeros[:], start=True, stop=True)
            pe.wait_ge(S["ident_ready"], 1)
            pe.wait_ge(S["h0_ready"], 1)
            turn(h0, S["h0_turned"], [ps_x])
            gate_sums(0)
            pe.wait_ge(S["h_t0"], 1)
            pe.wait_ge(S["ld_wkq"], 16)
            dense(ps_a[:], h_t, wkq).then_inc(S["kq_done"], 1)
            gate_sums(1)
            gate_sums(2)
            pe.wait_ge(S["kq_taken"], 1)
            turn(kq, S["kq_turned"], [ps_x])
            gate_sums(3)
            pe.wait_ge(S["kq_t_ready"], 1)
            pe.wait_ge(S["eq_ready"], 2)
            pe.wait_ge(S["ld_smalls"], 16)
            for c in range(2):
                pe.matmul(ps_c[:, 0:P], kq_t[:, 2 + c, :], kq_t[:, c, :], start=(c == 0), stop=(c == 1))
            for t in range(2):
                for c in range(2):
                    pe.matmul(ps_c[:, (1 + t) * P:(2 + t) * P], eq_b[:, c, t, :], kq_t[:, c, :], start=(c == 0), stop=(c == 1))
            for c in range(2):
                last = pe.matmul(ps_c[:, 3 * P:3 * P + 2], kq_t[:, 2 + c, :], smalls[:, EK + 2 * c:EK + 2 * c + 2],
                                 start=(c == 0), stop=(c == 1))
            last.then_inc(S["qk_done"], 1)
            pe.wait_ge(S["ld_wv"], 16)
            dense(ps_b[:], h_t, wv).then_inc(S["v_done"], 1)
            pe.wait_ge(S["prob_ready"], 1)
            pe.transpose(ps_x[:, 0:P], prob[:], ident[:])
            pe.wait_ge(S["mass_ready"], 2)
            pe.transpose(ps_x[0:2, P:2 * P], gate_mass[:], ident[:]).then_inc(S["p_turned"], 1)
            type_sums(0)
            pe.wait_ge(S["p_t_ready"], 2)
            pe.wait_ge(S["v_taken"], 1)
            pe.wait_ge(S["ld_ev"], 16)
            for i in range(2):
                h = slice(i * HALF, (i + 1) * HALF)
                pe.matmul(m_banks[i][:, 0:HALF], prob_t[:], v_sb[:, h], start=True, stop=False)
                pe.matmul(m_banks[i][:, 0:HALF], mass_t[:], ev[:, h], start=False, stop=True).then_inc(S["m_done"], 1)
            for c in range(1, 4):
                type_sums(c)
            pe.wait_ge(S["cen_ready"], 2)
            turn(cen, S["turned"], turned_banks[0])
            for c in range(4, EC):
                type_sums(c)

            def split_dense(out, k, l, start=True, stop=True):
                w = slot[k % SLOTS]
                pe.wait_ge(hi_ready, 2 * (k + 1))
                lo_wait(pe, k)
                for c in range(DC):
                    if c % 2 == 0:
                        pe.wait_ge(S["h_lo"], 2 * l + c // 2 + 1)
                    pe.matmul(out[:], h_hl[:, 0, c, :], w[:, 0, c, :], start=start and c == 0, stop=False)
                    pe.matmul(out[:], h_hl[:, 0, c, :], w[:, 1, c, :], start=False, stop=False)
                    last = pe.matmul(out[:], h_hl[:, 1, c, :], w[:, 0, c, :], start=False, stop=stop and c == DC - 1)
                last.then_inc(S["w_used"], 1)

            def bases(l):
                for b in range(BASES):
                    if l == 1 or b >= 2:
                        pe.wait_ge(S["hb_lo"], BASES * l + b - 1)
                    split_dense((ps_a, ps_b)[b % 2], (BASES + 1) * l + b, l)

            def aggregate(l, done):
                for i in range(2):
                    h = slice(i * HALF, (i + 1) * HALF)
                    for b in range(BASES):
                        pe.wait_ge(S["hb_lo"], BASES * l + b + 1)
                        pe.wait_ge(S["adj_lo"], l + 1)
                        a, m = adj_hl[l], hb_hl
                        out = agg_banks[i][:, 0:HALF]
                        pe.matmul(out, a[:, 0, b, :], m[:, 0, b, h], start=(b == 0), stop=False)
                        pe.matmul(out, a[:, 0, b, :], m[:, 1, b, h], start=False, stop=False)
                        last = pe.matmul(out, a[:, 1, b, :], m[:, 0, b, h], start=False, stop=(b == BASES - 1))
                    last.then_inc(done, 1)

            bases(0)
            split_dense(ps_c, 4, 0)
            aggregate(0, S["agg_done"])
            pe.wait_ge(S["h1_ready"], 2)
            turn(h1, S["turned"], turned_banks[1])
            bases(1)
            pe.wait_ge(S["adj_sum_ready"], 1)
            pe.wait_ge(S["norm_row_ready"], 1)
            pe.transpose(ps_sc[:, 0:P], adj_sum[:], ident[:])
            pe.transpose(ps_sc[:, P:2 * P], norm_row, ident[:]).then_inc(S["adj_turned"], 1)
            split_dense(ps_c, 9, 1)
            aggregate(1, S["conv_done"])
            pe.wait_ge(S["norm_t_ready"], 1)
            pe.wait_ge(S["adj_t_ready"], 1)
            pe.transpose(ps_sc[:, 2 * P:3 * P], norm_t, ident[:]).then_inc(S["norm_turned2"], 1)

            def gather(n):
                pe.wait_ge(S["scaled_ready"], n - 1)
                pe.wait_ge(S["cen_ready"], 2 * n)
                for c in range(DC):
                    last = pe.matmul(z_banks[c // 2][:, (c % 2) * P:(c % 2 + 1) * P], cen[:, c * P:(c + 1) * P], scaled[:, n - 2, :],
                                     start=True, stop=True)
                    if c % 2:
                        last.then_inc(S["z_done"], 1)

            pe.wait_ge(S["ones_ready"], 1)
            pe.wait_ge(S["ld_bias2"], 16)
            pe.wait_ge(S["ld_u"], 16)
            pe.wait_ge(S["ld_vt"], 16)
            gather(2)
            for c in range(DC):
                pe.wait_ge(S["z_taken"], c // 2 + 1)
                last = pe.matmul(ps_a[0:RANK, 0:P], u_w[:, c, :], z_t[:, c, :], start=(c == 0), stop=(c == DC - 1))
            last.then_inc(S["low_done"], 1)
            for i in range(2):
                pe.matmul(l2_banks[i][:, 0:HALF], ones[:], bias2[:, i * HALF:(i + 1) * HALF], start=True, stop=False)
            pe.wait_ge(S["low_taken"], 1)
            for i in range(2):
                h = slice(i * HALF, (i + 1) * HALF)
                pe.matmul(l2_banks[i][:, 0:HALF], low[:], vt_w[:, h], start=False, stop=True).then_inc(S["l2_done"], 1)
            pe.wait_ge(S["norm_ready"], 1)
            pe.wait_ge(S["ld_bias_b"], 48)
            for i in range(2):
                pe.matmul(l3_banks[i][:, 0:HALF], norm_adj[:], bias_b[:, 2, i * HALF:(i + 1) * HALF], start=True, stop=False)
            gather(3)
            pe.wait_ge(S["ld_w3"], 16)
            for i in range(2):
                h = slice(i * HALF, (i + 1) * HALF)
                pe.wait_ge(S["z_taken"], 4)
                dense(l3_banks[i][:, 0:HALF], z_t, w3, cols=h, start=False).then_inc(S["l3_done"], 1)


def kernel(**inputs):
    import numpy as np
    import concourse.bacc as bacc
    from concourse.bass_utils import run_bass_kernel_spmd

    i = {k: np.asarray(v) for k, v in inputs.items()}

    def rows(a):
        return np.broadcast_to(a.reshape(1, -1), (P, a.size))

    def halves(a):
        return a.reshape(2, 2, P).transpose(2, 1, 0).reshape(P, 4)

    pad = np.zeros((P, 1), np.float32)
    pad[:RANK, 0] = i["L2_gnn_s"]
    arrays = {
        "x": i["x"],
        "ints": np.stack([i[k].reshape(P, EC) for k in ("src", "dst", "edge_type_8")], axis=1),
        "smalls": np.concatenate([
            i["edge_weight"].reshape(P, EC), i["edge_weight1"].reshape(P, EC), halves(i["L0_gnn_Ek"]), halves(i["L0_gnn_Eq"]),
            rows(i["L0_gnn_idx_bias"]), rows(i["L0_gnn_idx_mult"]), rows(i["L1_gnn_comp0"]), rows(i["L1_gnn_comp1"]), pad], axis=1),
        "biases": np.stack([i["L1_gnn_bias0"], i["L1_gnn_bias1"], i["L3_gnn_b"], i["L2_gnn_bias"]]),
        "ev": i["L0_gnn_Ev"],
        "wkq": np.concatenate([i["L0_gnn_Wk"], i["L0_gnn_Wq"]], axis=1),
        "wv": i["L0_gnn_Wv"],
        "conv": np.concatenate([i["L1_gnn_basis0"], i["L1_gnn_loop0"][None], i["L1_gnn_basis1"], i["L1_gnn_loop1"][None]]),
        "u": i["L2_gnn_U"],
        "vt": i["L2_gnn_Vt"],
        "w3": i["L3_gnn_W"].T,
    }
    nc = bacc.Bacc("TRN2", target_bir_lowering=False, num_devices=1)
    args, maps = [], {}
    for name, a in arrays.items():
        a = np.ascontiguousarray(a)
        maps[f"in_{name}"] = a
        args.append(nc.dram_tensor(f"in_{name}", a.shape, mybir.dt.from_np(a.dtype), kind="ExternalInput").ap())
    args.append(nc.dram_tensor("out_0", (P, D), F32, kind="ExternalOutput").ap())
    gnn_stack(nc, *args)
    r = run_bass_kernel_spmd(nc, [maps], core_ids=[0])
    return r.results[0]["out_0"]
```

```python
from contextlib import ExitStack

import concourse.bass as bass
from concourse import mybir

ALU = mybir.AluOpType
ACT = mybir.ActivationFunctionType
AX_X = mybir.AxisListType.X
F32 = mybir.dt.float32
F32R = mybir.dt.float32r
I32 = mybir.dt.int32
BF16 = mybir.dt.bfloat16

P = 128
D = 512
DC = D // P
EC = 16
RELS = 8
BASES = 4
HID = 256
RANK = 64
LN_EPS = 1e-5
SCALE = float(D) ** -0.5
RING = 4
BATCH = 4
NB = EC // BATCH
TILES = 2 * (BASES + 1)
RAW = 5
SLOTS = 5
HALF = D // 2
WARM = 21
LO_ON_VECTOR = ((7, 0), (7, 1), (9, 1))

NORM, W1, EK, EQ, IDXB, IDXM, COMP0, COMP1, S2, SMALLS = 0, 16, 32, 36, 40, 41, 42, 74, 106, 107


def gnn_stack(nc: bass.Bass, x_d, ints_d, smalls_d, biases_d, ev_d, wkq_d, wv_d, conv_d, u_d, vt_d, w3_d, out_d):
    with ExitStack() as ctx:
        def sb(name, shape, dt=F32):
            return ctx.enter_context(nc.sbuf_tensor(name, shape, dt))

        def psum(name):
            return ctx.enter_context(nc.psum_tensor(name, [P, D], F32))

        def sem(name):
            return ctx.enter_context(nc.semaphore(name))

        ps_t = [psum("ps_t0"), psum("ps_t1")]
        ps_sc = psum("ps_sc")
        ps_x = psum("ps_x")
        ps_a = psum("ps_a")
        ps_b = psum("ps_b")
        ps_c = psum("ps_c")
        ps_o = psum("ps_o")
        m_banks = (ps_o, ps_c)
        turned_banks = ((ps_x, ps_o), (ps_x, ps_t[1]))
        agg_banks = (ps_o, ps_t[0])
        z_banks = (ps_x, ps_t[1])
        l2_banks = (ps_b, ps_a)
        l3_banks = (ps_c, ps_o)

        raw = [sb(f"raw{i}", [P, DC, D]) for i in range(RAW)]
        slot = [sb(f"slot{i}", [P, 2, DC, D], F32R) for i in range(SLOTS)]
        u_w = sb("u_w", [P, DC, RANK])
        vt_w = sb("vt_w", [RANK, D])
        bias_b = sb("bias_b", [P, 3, D])
        bias2 = sb("bias2", [1, D])
        ev = sb("ev", [2, D])
        wkq, wv = raw[0], raw[1]

        ints = sb("ints", [P, 3, EC], I32)
        smalls = sb("smalls", [P, SMALLS])
        iota = sb("iota", [P, RELS * P])
        ident = sb("ident", [P, P])
        zeros = sb("zeros", [P, HALF], BF16)
        ones = sb("ones", [1, P])
        eq_b = sb("eq_b", [P, 2, 2, P])
        ends = sb("ends", [P, 3, EC])
        norm_hl = sb("norm_hl", [P, 2, EC], F32R)
        gate = sb("gate", [P, 4, EC])
        gate_hl = sb("gate_hl", [P, 2, EC], F32R)
        hb_flat = sb("hb_flat", [P, 2 * BASES * D], F32R)
        src_oh = hb_flat[:, 0:EC * P].rearrange("p (c n) -> p c n", c=EC)
        src_n01 = hb_flat[:, EC * P:2 * EC * P].rearrange("p (k j b n) -> p k j b n", k=2, j=2, b=BATCH)
        src_n2 = sb("src_n2", [P, 2, BATCH, P], F32R)
        src_n = [src_n01[:, 0, :, :, :], src_n01[:, 1, :, :, :], src_n2[:]]
        hb_hl = hb_flat[:].rearrange("p (j b n) -> p j b n", j=2, b=BASES)
        dst_oh = slot[3][:].rearrange("p a c n -> p a (c n)").rearrange("p a (c n) -> p a c n", c=EC)
        dst_lo = slot[2][:, 0, :, :].rearrange("p c n -> p (c n)").rearrange("p (c n) -> p c n", c=EC)
        key_oh = slot[4][:].rearrange("p a c n -> p (a c n)").rearrange("p (r n) -> p r n", r=RING)

        cnt_s = sb("cnt_s", [P, 2, P])
        gate_c = sb("gate_c", [P, P])
        t_sb = sb("t_sb", [P, RELS, P])
        adj = sb("adj", [P, BASES, P])
        adj_hl = [sb(f"adj_hl{l}", [P, 2, BASES, P], F32R) for l in range(2)]
        adj_t = sb("adj_t", [P, P])
        cnt_i = sb("cnt_i", [P, P])
        norm_adj = sb("norm_adj", [P, P])
        deg = sb("deg", [P, 3])

        x0 = sb("x0", [P, D])
        stats = sb("stats", [P, 8])
        table = sb("table", [P, 1])
        half = sb("half", [P, 3, 2, 6])
        moments = sb("moments", [P, 3, 2])
        eps = sb("eps", [P, 1])
        std = sb("std", [P, 4])
        rstd = sb("rstd", [P, 4])
        cen = sb("cen", [P, D])
        h_t = sb("h_t", [P, DC, P])
        h_hl = sb("h_hl", [P, 2, DC, P], F32R)
        kq = sb("kq", [P, D])
        kq_t = sb("kq_t", [P, 4, P])
        v_sb = sb("v_sb", [P, D])
        bias_s = sb("bias_s", [P, 2, P])
        att = sb("att", [P, 2, P])
        row_max = sb("row_max", [P, 2])
        prob = sb("prob", [P, P])
        prob_s = sb("prob_s", [P, 2, P])
        row_sum = sb("row_sum", [P, 2])
        gate_mass = sb("gate_mass", [P, 2])
        prob_t = sb("prob_t", [P, P])
        mass_t = sb("mass_t", [2, P])
        x1 = sb("x1", [P, D])
        x1_bias = sb("x1_bias", [P, D])
        x2 = sb("x2", [P, D])
        low = sb("low", [RANK, P])
        scaled, norm_row, norm_t = att, bias_s[:, 0, :], bias_s[:, 1, :]
        h0, h1, loop_sb, x3, x4, z_t = x1, kq, v_sb, kq, v_sb, h_t

        names = """eps_ready half_stats ld_ints ld_smalls ld_x ld_bias_b ld_bias2 ld_ev ld_wv ld_u ld_vt
            iota_ready ident_ready ones_ready var0 std0 h0_ready h0_turned h_t0 ends_ready norm_hl_ready gate_z gate_e
            gate_hl_ready src_rows dst_rows gate_hi_rows gate_lo_rows warm_ready sc_used sc_taken src_n_rows key_rows t_half t_used t_taken
            kq_done kq_taken v_done v_taken kq_turned kq_t_ready
            eq_ready qk_done att_max prob_ready mass_ready p_turned p_t_ready m_done x_ready x1_bias_ready
            var_ready std_ready rstd_ready cen_ready turned h_hi h_lo hb_hi hb_lo
            loop_taken adj_mix adj_hi adj_lo agg_done h1_ready conv_done
            adj_sum adj_t_ready deg_ready deg_std deg_inverse norm_row_ready norm_t_ready
            norm_turned later_turned norm_ready scaled_ready z_done z_taken low_done low_taken l2_done
            l3_done x4_ready stored w_used chain_v chain_g""".split()
        S = {n: sem(n) for n in names}
        ld_tile = [sem(f"ld_tile{k}") for k in range(TILES + 1)]
        ld_wkq = [sem("ld_wkq0"), sem("ld_wkq1")]
        hi_ready = sem("hi_ready")
        lo_by_vector = sem("lo_by_vector")
        lo_by_pool = sem("lo_by_pool")

        def lo_wait(eng, k):
            by_vector = [j for j, _ in LO_ON_VECTOR if j <= k]
            if k in by_vector:
                eng.wait_ge(lo_by_vector, len(by_vector))
            if by_vector.count(k) < 2:
                eng.wait_ge(lo_by_pool, 2 * (k + 1) - len(by_vector))

        def raw_of(k):
            return raw[(2 + k) % RAW]

        block = ctx.enter_context(nc.Block())

        @block.sync
        def _(sp):
            sp.dma_start(ints[:], ints_d).then_inc(S["ld_ints"], 16)
            sp.dma_start(x0[:], x_d).then_inc(S["ld_x"], 16)
            sp.dma_start(smalls[:], smalls_d).then_inc(S["ld_smalls"], 16)
            for i in range(2):
                sp.dma_start(wkq[:, 2 * i:2 * i + 2, :], wkq_d[i * HALF:(i + 1) * HALF, :].rearrange("(c p) n -> p c n", p=P)).then_inc(ld_wkq[i], 16)
            sp.dma_start(wv[:], wv_d.rearrange("(c p) n -> p c n", p=P)).then_inc(S["ld_wv"], 16)
            sp.dma_start(ev[:], ev_d).then_inc(S["ld_ev"], 16)
            for k in range(TILES + 1):
                if k == RAW - 2:
                    sp.wait_ge(S["kq_done"], 1)
                if k == RAW - 1:
                    sp.wait_ge(S["v_done"], 1)
                if k >= RAW:
                    sp.wait_ge(hi_ready, 2 * (k - RAW + 1))
                    lo_wait(sp, k - RAW)
                w_d = conv_d[k] if k < TILES else w3_d
                sp.dma_start(raw_of(k)[:], w_d.rearrange("(c p) n -> p c n", p=P)).then_inc(ld_tile[k], 16)
                if k == 4:
                    for j in range(3):
                        sp.dma_start(bias_b[:, j, :], biases_d[j:j + 1, :].broadcast_to([P, D])).then_inc(S["ld_bias_b"], 16)
                    sp.dma_start(bias2[:], biases_d[3:4, :]).then_inc(S["ld_bias2"], 16)
                    sp.dma_start(u_w[:], u_d.rearrange("(c p) n -> p c n", p=P)).then_inc(S["ld_u"], 16)
                    sp.dma_start(vt_w[:], vt_d).then_inc(S["ld_vt"], 16)
            for i in range(2):
                sp.wait_ge(S["x4_ready"], i + 1)
                sp.dma_start(out_d[:, i * HALF:(i + 1) * HALF], x4[:, i * HALF:(i + 1) * HALF]).then_inc(S["stored"], 16)
            sp.wait_ge(S["stored"], 32)

        def slot_free(eng, k):
            if k in (2, 3):
                eng.wait_ge(S["sc_used"], EC)
            if k == 4:
                eng.wait_ge(S["t_used"], EC)
            if k >= SLOTS:
                eng.wait_ge(S["w_used"], k - SLOTS + 1)

        def low_part(eng, k, i, done):
            eng.wait_ge(hi_ready, 2 * k + i + 1)
            slot_free(eng, k)
            c = slice(2 * i, 2 * i + 2)
            eng.tensor_tensor(slot[k % SLOTS][:, 1, c, :].rearrange("p c n -> p (c n)"), raw_of(k)[:, c, :].rearrange("p c n -> p (c n)"),
                              slot[k % SLOTS][:, 0, c, :].rearrange("p c n -> p (c n)").bitcast(F32), ALU.subtract).then_inc(done, 1)

        @block.gpsimd
        def _(pool):
            pool.iota(iota[:], pattern=[[1, RELS * P]], base=0, channel_multiplier=0,
                      allow_small_or_imprecise_dtypes=True).then_inc(S["iota_ready"], 1)
            pool.memset(ident[:], 0.0).then_inc(S["chain_g"], 1)
            pool.wait_ge(S["chain_g"], 1)
            pool.affine_select(out=ident[:], in_=ident[:], compare_op=ALU.not_equal, fill=1.0, base=0,
                               pattern=[[-1, P]], channel_multiplier=1).then_inc(S["ident_ready"], 1)
            pool.memset(ones[:], 1.0).then_inc(S["ones_ready"], 1)
            for b in range(NB):
                if b == 0:
                    pool.wait_ge(S["norm_hl_ready"], 2)
                pool.wait_ge(S["src_rows"], b + 1)
                if b >= 3:
                    for k in range(2):
                        for i in range(2):
                            low_part(pool, k, i, lo_by_pool)
                    pool.wait_ge(S["t_used"], BATCH * (b - 2))
                for j in range(2):
                    w = norm_hl[:, j, b * BATCH:(b + 1) * BATCH].bitcast(F32).rearrange("p (b o) -> p b o", o=1)
                    pool.tensor_tensor(src_n[b % 3][:, j, :, :], src_oh[:, b * BATCH:(b + 1) * BATCH, :].bitcast(F32),
                                       w.broadcast_to([P, BATCH, P]), ALU.mult).then_inc(S["src_n_rows"], 1)
            for k in range(2, TILES + 1):
                if k == TILES:
                    pool.wait_ge(S["adj_mix"], 2 * BASES * RELS)
                    for s, n in enumerate((4, 2, 1)):
                        if s:
                            pool.wait_ge(S["adj_sum"], s)
                        pool.tensor_tensor(t_sb[:, 0:n, :], t_sb[:, 0:n, :], t_sb[:, n:2 * n, :], ALU.add).then_inc(S["adj_sum"], 1)
                for i in range(2):
                    if (k, i) not in LO_ON_VECTOR:
                        low_part(pool, k, i, lo_by_pool)
                if k == 4:
                    pool.wait_ge(S["x_ready"], 2)
                    pool.wait_ge(S["ld_bias_b"], 48)
                    pool.tensor_tensor(x1_bias[:], x1[:], bias_b[:, 1, :], ALU.add).then_inc(S["x1_bias_ready"], 1)

        @block.scalar
        def _(act):
            act.wait_ge(S["var0"], 1)
            act.activation(std[:, 0:1], stats[:, 7:8], ACT.Sqrt, bias=eps[:]).then_inc(S["std0"], 1)
            act.wait_ge(S["gate_z"], 1)
            act.activation(gate[:, 1, :], gate[:, 0, :], ACT.Exp, scale=-1.0).then_inc(S["gate_e"], 1)

            def gate_lo(c):
                b = c // BATCH
                act.wait_ge(S["dst_rows"], b + 1)
                if c == 0:
                    act.wait_ge(S["gate_hl_ready"], 2)
                act.activation(dst_lo[:, c, :], dst_oh[:, 0, c, :].bitcast(F32), ACT.Copy,
                               scale=gate_hl[:, 1, c:c + 1].bitcast(F32)).then_inc(S["gate_lo_rows"], 1)

            for i in range(2):
                act.wait_ge(S["h0_turned"], i + 1)
                act.activation(h_t[:, 2 * i:2 * i + 2, :].rearrange("p c n -> p (c n)"), turned_banks[0][i][:, 0:HALF],
                               ACT.Relu).then_inc(S["h_t0"], 1)
            for c in range(2 * BATCH):
                gate_lo(c)
            act.wait_ge(S["kq_done"], 1)
            act.copy(kq[:], ps_a[:]).then_inc(S["kq_taken"], 1)
            for c in range(2 * BATCH, EC):
                gate_lo(c)

            def high_part(k, halves=(0, 1)):
                act.wait_ge(ld_tile[k], 16)
                slot_free(act, k)
                for i in halves:
                    act.copy(slot[k % SLOTS][:, 0, 2 * i:2 * i + 2, :].rearrange("p c n -> p (c n)"),
                             raw_of(k)[:, 2 * i:2 * i + 2, :].rearrange("p c n -> p (c n)")).then_inc(hi_ready, 1)

            act.wait_ge(S["kq_turned"], 1)
            act.copy(kq_t[:].rearrange("p c n -> p (c n)"), ps_x[:]).then_inc(S["kq_t_ready"], 1)
            high_part(0)
            high_part(1, [0])
            act.wait_ge(S["att_max"], 1)
            act.activation(prob[:], att[:, 1, :], ACT.Exp, bias=row_max[:, 1:2], scale=SCALE,
                           accum_out=row_sum[:, 0:1]).then_inc(S["prob_ready"], 1)
            high_part(1, [1])
            act.wait_ge(S["v_done"], 1)
            act.copy(v_sb[:], ps_b[:]).then_inc(S["v_taken"], 1)
            act.wait_ge(S["p_turned"], 1)
            act.copy(prob_t[:], ps_x[:, 0:P]).then_inc(S["p_t_ready"], 1)
            act.copy(mass_t[:], ps_x[0:2, P:2 * P]).then_inc(S["p_t_ready"], 1)
            act.wait_ge(S["warm_ready"], 1)
            act.activation(table[:], zeros[:, 0:1], ACT.Sqrt)

            def root(n):
                act.wait_ge(S["var_ready"], n)
                act.activation(std[:, n:n + 1], moments[:, n - 1, 1:2], ACT.Sqrt, bias=eps[:]).then_inc(S["std_ready"], 1)

            def turned_high(n):
                for i in range(2):
                    act.wait_ge(S["turned"], 2 * (n - 1) + i + 1)
                    act.activation(h_hl[:, 0, 2 * i:2 * i + 2, :].rearrange("p c n -> p (c n)"), turned_banks[n - 1][i][:, 0:HALF],
                                   ACT.Relu).then_inc(S["h_hi"], 1)

            def basis_high(l, b):
                act.wait_ge(S["w_used"], (BASES + 1) * l + b + 1)
                if l == 1 and b == 0:
                    act.wait_ge(S["agg_done"], 2)
                ps = (ps_a, ps_b)[b % 2]
                if l == 0:
                    act.activation(hb_hl[:, 0, b, :], ps[:], ACT.Copy, scale=rstd[:, 1:2]).then_inc(S["hb_hi"], 1)
                else:
                    act.copy(hb_hl[:, 0, b, :], ps[:]).then_inc(S["hb_hi"], 1)

            def mix_high(l):
                for i in range(2):
                    act.wait_ge(S["adj_mix"], BASES * (RELS * (l + 1) - 1) + 2 * i + 2)
                    act.copy(adj_hl[l][:, 0, 2 * i:2 * i + 2, :].rearrange("p b n -> p (b n)"),
                             adj[:, 2 * i:2 * i + 2, :].rearrange("p b n -> p (b n)")).then_inc(S["adj_hi"], 1)

            turned_high(1)
            root(1)
            act.wait_ge(S["deg_ready"], 1)
            act.activation(deg[:, 1:2], deg[:, 0:1], ACT.Sqrt).then_inc(S["deg_std"], 1)
            high_part(2)
            high_part(3)
            act.wait_ge(S["t_half"], 1)
            for i in range(2):
                if i == 1:
                    act.wait_ge(S["t_used"], EC)
                act.copy(t_sb[:, 4 * i:4 * i + 4, :].rearrange("p r n -> p (r n)"), ps_t[i][:]).then_inc(S["t_taken"], 1)
            high_part(4)
            act.wait_ge(S["rstd_ready"], 1)
            basis_high(0, 0)
            high_part(5)
            basis_high(0, 1)
            high_part(6)
            basis_high(0, 2)
            high_part(7)
            basis_high(0, 3)
            mix_high(0)
            high_part(8)
            turned_high(2)
            high_part(9)
            act.wait_ge(S["norm_turned"], 1)
            act.activation(norm_t, ps_sc[:, P:2 * P], ACT.Copy, scale=deg[:, 2:3]).then_inc(S["norm_t_ready"], 1)
            basis_high(1, 0)
            basis_high(1, 1)
            basis_high(1, 2)
            mix_high(1)
            basis_high(1, 3)
            high_part(TILES)

            act.wait_ge(S["later_turned"], 1)
            act.copy(adj_t[:], ps_sc[:, 0:P]).then_inc(S["adj_t_ready"], 1)
            act.copy(norm_adj[:], ps_sc[:, 2 * P:3 * P]).then_inc(S["norm_ready"], 1)
            root(2)
            for i in range(2):
                act.wait_ge(S["z_done"], i + 1)
                act.copy(z_t[:, 2 * i:2 * i + 2, :].rearrange("p c n -> p (c n)"), z_banks[i][:, 0:HALF]).then_inc(S["z_taken"], 1)
            act.wait_ge(S["low_done"], 1)
            act.activation(low[:], ps_c[0:RANK, 0:P], ACT.Copy, scale=smalls[0:RANK, S2:S2 + 1]).then_inc(S["low_taken"], 1)
            root(3)
            for i in range(2):
                act.wait_ge(S["z_done"], 2 + i + 1)
                act.copy(h_hl[:, 0, 2 * i:2 * i + 2, :].rearrange("p c n -> p (c n)"), z_banks[i][:, 0:HALF]).then_inc(S["h_hi"], 1)

        @block.vector
        def _(dve):
            chain = [0]

            def link(ins):
                chain[0] += 1
                ins.then_inc(S["chain_v"], 1)
                dve.wait_ge(S["chain_v"], chain[0])

            def spread(a):
                return a.rearrange("p (b o) -> p b o", o=1).broadcast_to([P, BATCH, P])

            def batch_rows(b, part):
                cs = slice(b * BATCH, (b + 1) * BATCH)
                columns = iota[:, 0:P].rearrange("p (o n) -> p o n", o=1).broadcast_to([P, BATCH, P])
                if part == 0:
                    dve.tensor_tensor(src_oh[:, cs, :], columns, spread(ends[:, 0, cs]), ALU.is_equal).then_inc(S["src_rows"], 1)
                if part == 1:
                    dve.tensor_tensor(dst_oh[:, 0, cs, :], columns, spread(ends[:, 1, cs]), ALU.is_equal).then_inc(S["dst_rows"], 1)
                if part == 2:
                    dve.wait_ge(S["dst_rows"], b + 1)
                    dve.tensor_tensor(dst_oh[:, 1, cs, :], dst_oh[:, 0, cs, :].bitcast(F32),
                                      spread(gate_hl[:, 0, cs].bitcast(F32)), ALU.mult).then_inc(S["gate_hi_rows"], 1)

            def type_rows(c):
                if c >= RING:
                    dve.wait_ge(S["t_used"], c - RING + 1)
                dve.tensor_scalar(key_oh[:, c % RING, :], iota[:], ends[:, 2, c:c + 1], None, ALU.is_equal).then_inc(S["key_rows"], 1)

            dve.memset(zeros[:], 0.0).then_inc(S["warm_ready"], 1)
            dve.memset(eps[:], LN_EPS).then_inc(S["eps_ready"], 1)
            dve.wait_ge(S["ld_ints"], 16)
            dve.tensor_copy(ends[:, 0:2, :], ints[:, 0:2, :]).then_inc(S["ends_ready"], 1)
            dve.scalar_tensor_tensor(ends[:, 2, :], ints[:, 2, :], float(P), ints[:, 1, :], ALU.mult, ALU.add).then_inc(S["ends_ready"], 1)
            dve.wait_ge(S["iota_ready"], 1)
            dve.wait_ge(S["ends_ready"], 1)
            batch_rows(0, 0)
            dve.wait_ge(S["ld_x"], 16)
            link(dve.bn_stats(stats[:, 0:6], x0[:]))
            dve.wait_ge(S["eps_ready"], 1)
            dve.bn_aggr(stats[:, 6:8], stats[:, 0:6]).then_inc(S["var0"], 1)
            dve.wait_ge(S["ld_smalls"], 16)
            dve.tensor_scalar(gate[:, 0, :], smalls[:, W1:W1 + EC], smalls[:, IDXB:IDXB + 1], smalls[:, IDXM:IDXM + 1],
                              ALU.subtract, ALU.mult).then_inc(S["gate_z"], 1)
            dve.tensor_copy(norm_hl[:, 0, :], smalls[:, NORM:NORM + EC]).then_inc(S["norm_hl_ready"], 1)
            dve.wait_ge(S["std0"], 1)
            link(dve.reciprocal(rstd[:, 0:1], std[:, 0:1]))
            for i in range(2):
                h = slice(i * HALF, (i + 1) * HALF)
                dve.tensor_scalar(h0[:, h], x0[:, h], stats[:, 6:7], rstd[:, 0:1], ALU.subtract, ALU.mult).then_inc(S["h0_ready"], 1)
            dve.wait_ge(S["norm_hl_ready"], 1)
            dve.tensor_tensor(norm_hl[:, 1, :], smalls[:, NORM:NORM + EC], norm_hl[:, 0, :].bitcast(F32),
                              ALU.subtract).then_inc(S["norm_hl_ready"], 1)
            batch_rows(0, 1)
            dve.wait_ge(S["gate_e"], 1)
            link(dve.tensor_scalar(gate[:, 2, :], gate[:, 1, :], 3e38, 1.0, ALU.min, ALU.add))
            link(dve.reciprocal(gate[:, 3, :], gate[:, 2, :]))
            dve.tensor_copy(gate_hl[:, 0, :], gate[:, 3, :]).then_inc(S["gate_hl_ready"], 1)
            dve.wait_ge(S["gate_hl_ready"], 1)
            dve.tensor_tensor(gate_hl[:, 1, :], gate[:, 3, :], gate_hl[:, 0, :].bitcast(F32), ALU.subtract).then_inc(S["gate_hl_ready"], 1)
            batch_rows(0, 2)
            for b in range(1, NB):
                for part in range(3):
                    batch_rows(b, part)
            for t in range(2):
                dve.tensor_copy(eq_b[:, :, t, :], smalls[:, EQ + t:EQ + 4:2].rearrange("p (c o) -> p c o", o=1)
                                .broadcast_to([P, 2, P])).then_inc(S["eq_ready"], 1)
            dve.wait_ge(S["ends_ready"], 2)
            for c in range(3):
                type_rows(c)
            dve.wait_ge(S["sc_used"], EC)
            link(dve.tensor_copy(cnt_s[:].rearrange("p a n -> p (a n)"), ps_sc[:, 0:2 * P]))
            dve.tensor_tensor(gate_c[:], cnt_s[:, 0, :], cnt_s[:, 1, :], ALU.subtract).then_inc(S["sc_taken"], 1)
            type_rows(3)
            dve.wait_ge(S["qk_done"], 1)
            dve.wait_ge(S["sc_taken"], 1)
            dve.scalar_tensor_tensor(bias_s[:, 0, :], ps_c[:, P:2 * P], ps_c[:, 3 * P:3 * P + 1], cnt_s[:, 1, :], ALU.add, ALU.mult)
            link(dve.scalar_tensor_tensor(bias_s[:, 1, :], ps_c[:, 2 * P:3 * P], ps_c[:, 3 * P + 1:3 * P + 2], gate_c[:], ALU.add, ALU.mult))
            link(dve.scalar_tensor_tensor(att[:, 0, :], ps_c[:, 0:P], 2.0, bias_s[:, 0, :], ALU.mult, ALU.add))
            link(dve.tensor_tensor_reduce(out=att[:, 1, :], in0=att[:, 0, :], in1=bias_s[:, 1, :], scale=1.0, scalar=-3e38,
                                          op0=ALU.add, op1=ALU.max, accum_out=row_max[:, 0:1]))
            dve.tensor_scalar(row_max[:, 1:2], row_max[:, 0:1], -SCALE, None, ALU.mult).then_inc(S["att_max"], 1)
            dve.wait_ge(S["prob_ready"], 1)
            dve.tensor_tensor_reduce(out=prob_s[:, 0, :], in0=prob[:], in1=cnt_s[:, 1, :], scale=1.0, scalar=0.0,
                                     op0=ALU.mult, op1=ALU.add, accum_out=gate_mass[:, 0:1]).then_inc(S["mass_ready"], 1)
            dve.tensor_tensor_reduce(out=prob_s[:, 1, :], in0=prob[:], in1=gate_c[:], scale=1.0, scalar=0.0,
                                     op0=ALU.mult, op1=ALU.add, accum_out=gate_mass[:, 1:2]).then_inc(S["mass_ready"], 1)
            link(dve.reciprocal(row_sum[:, 1:2], row_sum[:, 0:1]))
            type_rows(4)
            type_rows(5)

            def half_stats(n, i, x):
                dve.wait_ge(S["x_ready"], 2 * n - 1 + i)
                dve.bn_stats(half[:, n - 1, i, :], x[:, i * HALF:(i + 1) * HALF]).then_inc(S["half_stats"], 1)

            def normal(n, x, adjacency=None):
                dve.wait_ge(S["half_stats"], 2 * n)
                dve.bn_aggr(moments[:, n - 1, :], half[:, n - 1, :, :]).then_inc(S["var_ready"], 1)
                dve.wait_ge(S["var_ready"], n)
                for i in range(2):
                    h = slice(i * HALF, (i + 1) * HALF)
                    if i == 1 and adjacency:
                        inverse(n)
                        dve.wait_ge(S["rstd_ready"], n)
                        dve.tensor_scalar(scaled[:, n - 2, :], adjacency[:], rstd[:, n:n + 1], None, ALU.mult).then_inc(S["scaled_ready"], 1)
                    dve.tensor_scalar(cen[:, h], x[:, h], moments[:, n - 1, 0:1], 0.0 if adjacency else None, ALU.subtract,
                                      ALU.max if adjacency else ALU.bypass).then_inc(S["cen_ready"], 1)

            def inverse(n):
                dve.wait_ge(S["std_ready"], n)
                dve.reciprocal(rstd[:, n:n + 1], std[:, n:n + 1]).then_inc(S["rstd_ready"], 1)

            def turned_low(n):
                for i in range(2):
                    dve.wait_ge(S["h_hi"], 2 * (n - 1) + i + 1)
                    dve.scalar_tensor_tensor(h_hl[:, 1, 2 * i:2 * i + 2, :].rearrange("p c n -> p (c n)"), turned_banks[n - 1][i][:, 0:HALF],
                                             0.0, h_hl[:, 0, 2 * i:2 * i + 2, :].rearrange("p c n -> p (c n)").bitcast(F32),
                                             ALU.max, ALU.subtract).then_inc(S["h_lo"], 1)

            def basis_low(l, b):
                dve.wait_ge(S["hb_hi"], BASES * l + b + 1)
                dve.wait_ge(S["rstd_ready"], 1)
                ps = (ps_a, ps_b)[b % 2]
                dve.scalar_tensor_tensor(hb_hl[:, 1, b, :], ps[:], rstd[:, 1:2] if l == 0 else 1.0, hb_hl[:, 0, b, :].bitcast(F32),
                                         ALU.mult, ALU.subtract).then_inc(S["hb_lo"], 1)

            def mix(l, rels):
                if l == 1 and 0 in rels:
                    dve.wait_ge(S["adj_hi"], 2)
                    dve.wait_ge(S["adj_lo"], 2)
                comp = (COMP0, COMP1)[l]
                for r in rels:
                    for b in range(BASES):
                        if r > 0:
                            dve.wait_ge(S["adj_mix"], BASES * (RELS * l + r - 1) + b + 1)
                        k = comp + r * BASES + b
                        if r == 0:
                            ins = dve.tensor_scalar(adj[:, b, :], t_sb[:, r, :], smalls[:, k:k + 1], None, ALU.mult)
                        else:
                            ins = dve.scalar_tensor_tensor(adj[:, b, :], t_sb[:, r, :], smalls[:, k:k + 1], adj[:, b, :], ALU.mult, ALU.add)
                        ins.then_inc(S["adj_mix"], 1)

            def mix_low(l):
                for i in range(2):
                    dve.wait_ge(S["adj_hi"], 2 * l + i + 1)
                    b = slice(2 * i, 2 * i + 2)
                    dve.tensor_tensor(adj_hl[l][:, 1, b, :].rearrange("p b n -> p (b n)"), adj[:, b, :].rearrange("p b n -> p (b n)"),
                                      adj_hl[l][:, 0, b, :].rearrange("p b n -> p (b n)").bitcast(F32), ALU.subtract).then_inc(S["adj_lo"], 1)

            for i in range(2):
                h = slice(i * HALF, (i + 1) * HALF)
                dve.wait_ge(S["m_done"], i + 1)
                dve.scalar_tensor_tensor(x1[:, h], m_banks[i][:, 0:HALF], row_sum[:, 1:2], x0[:, h], ALU.mult, ALU.add).then_inc(S["x_ready"], 1)
                half_stats(1, i, x1)
            normal(1, x1)
            for c in range(6, 8):
                type_rows(c)
            turned_low(1)
            type_rows(8)
            type_rows(9)
            dve.scalar_tensor_tensor(cnt_i[:], cnt_s[:, 0, :], 1.0, ident[:], ALU.mult, ALU.add, accum_out=deg[:, 0:1]).then_inc(S["deg_ready"], 1)
            type_rows(10)
            inverse(1)
            dve.wait_ge(S["deg_std"], 1)
            dve.reciprocal(deg[:, 2:3], deg[:, 1:2]).then_inc(S["deg_inverse"], 1)
            type_rows(11)
            dve.wait_ge(S["deg_inverse"], 1)
            dve.tensor_scalar(norm_row, cnt_i[:], deg[:, 2:3], None, ALU.mult).then_inc(S["norm_row_ready"], 1)
            for c in range(12, EC):
                type_rows(c)
            dve.wait_ge(S["t_taken"], 1)
            mix(0, range(0, 4))
            dve.wait_ge(S["t_taken"], 2)
            basis_low(0, 0)
            mix(0, range(4, 6))
            basis_low(0, 1)
            mix(0, range(6, 8))
            basis_low(0, 2)
            low_part(dve, 7, 0, lo_by_vector)
            basis_low(0, 3)
            mix_low(0)
            low_part(dve, 7, 1, lo_by_vector)
            dve.wait_ge(S["w_used"], BASES + 1)
            dve.wait_ge(S["ld_bias_b"], 48)
            dve.scalar_tensor_tensor(loop_sb[:], ps_c[:], rstd[:, 1:2], bias_b[:, 0, :], ALU.mult, ALU.add).then_inc(S["loop_taken"], 1)
            dve.wait_ge(S["loop_taken"], 1)
            for i in range(2):
                if i == 1:
                    mix(1, range(0, 1))
                h = slice(i * HALF, (i + 1) * HALF)
                dve.wait_ge(S["agg_done"], i + 1)
                dve.tensor_tensor(h1[:, h], agg_banks[i][:, 0:HALF], loop_sb[:, h], ALU.add).then_inc(S["h1_ready"], 1)
            turned_low(2)
            mix(1, range(1, 2))
            low_part(dve, 9, 1, lo_by_vector)
            basis_low(1, 0)
            mix(1, range(2, 4))
            basis_low(1, 1)
            mix(1, range(4, 6))
            basis_low(1, 2)
            mix(1, range(6, 8))
            mix_low(1)
            basis_low(1, 3)
            dve.wait_ge(S["x1_bias_ready"], 1)
            dve.wait_ge(S["w_used"], TILES)
            dve.tensor_tensor(loop_sb[:], ps_c[:], x1_bias[:], ALU.add).then_inc(S["loop_taken"], 1)
            dve.wait_ge(S["loop_taken"], 2)
            for i in range(2):
                h = slice(i * HALF, (i + 1) * HALF)
                dve.wait_ge(S["conv_done"], i + 1)
                dve.tensor_tensor(x2[:, h], agg_banks[i][:, 0:HALF], loop_sb[:, h], ALU.add).then_inc(S["x_ready"], 1)
                half_stats(2, i, x2)
            dve.wait_ge(S["adj_t_ready"], 1)
            normal(2, x2, adj_t)
            for i in range(2):
                h = slice(i * HALF, (i + 1) * HALF)
                dve.wait_ge(S["l2_done"], i + 1)
                dve.scalar_tensor_tensor(x3[:, h], l2_banks[i][:, 0:HALF], 0.0, x2[:, h], ALU.max, ALU.add).then_inc(S["x_ready"], 1)
            for i in range(2):
                half_stats(3, i, x3)
            dve.wait_ge(S["norm_ready"], 1)
            normal(3, x3, norm_adj)
            for i in range(2):
                dve.wait_ge(S["h_hi"], 4 + i + 1)
                dve.tensor_tensor(h_hl[:, 1, 2 * i:2 * i + 2, :].rearrange("p c n -> p (c n)"), z_banks[i][:, 0:HALF],
                                  h_hl[:, 0, 2 * i:2 * i + 2, :].rearrange("p c n -> p (c n)").bitcast(F32),
                                  ALU.subtract).then_inc(S["h_lo"], 1)
            for i in range(2):
                h = slice(i * HALF, (i + 1) * HALF)
                dve.wait_ge(S["l3_done"], i + 1)
                dve.scalar_tensor_tensor(x4[:, h], l3_banks[i][:, 0:HALF], 0.0, x3[:, h], ALU.max, ALU.add).then_inc(S["x4_ready"], 1)

        @block.tensor
        def _(pe):
            def values(c):
                return pe.matmul(ps_b[:], h_t[:, c, :], wv[:, c, :], start=(c == 0), stop=(c == DC - 1))

            def turn(src, done, banks, ready, before):
                n = DC // len(banks)
                for i, bank in enumerate(banks):
                    pe.wait_ge(ready, before + i + 1)
                    for c in range(n):
                        last = pe.transpose(bank[:, c * P:(c + 1) * P], src[:, (i * n + c) * P:(i * n + c + 1) * P], ident[:])
                    last.then_inc(done, 1)

            def type_sums(c, groups=(0, 1)):
                b = c // BATCH
                pe.wait_ge(S["src_n_rows"], 2 * (b + 1))
                pe.wait_ge(S["key_rows"], c + 1)
                for j in range(2):
                    for i in groups:
                        last = pe.matmul(ps_t[i][:], src_n[b % 3][:, j, c % BATCH, :], key_oh[:, c % RING, i * 512:(i + 1) * 512],
                                         start=(c == 0 and j == 0), stop=(c == EC - 1 and j == 1))
                if 1 in groups:
                    last.then_inc(S["t_used"], 1)
                elif c == EC - 1:
                    last.then_inc(S["t_half"], 1)

            def gate_sums(b):
                for c in range(BATCH * b, BATCH * (b + 1)):
                    s = src_oh[:, c, :]
                    d = dst_oh[:, :, c, :]
                    pe.wait_ge(S["gate_hi_rows"], b + 1)
                    if c < EC - 1:
                        pe.matmul(ps_sc[:, 0:2 * P], s, d, start=(c == 0), stop=False)
                    pe.wait_ge(S["gate_lo_rows"], c + 1)
                    last = pe.matmul(ps_sc[:, P:2 * P], s, dst_lo[:, c, :], start=False, stop=False)
                    if c == EC - 1:
                        last = pe.matmul(ps_sc[:, 0:2 * P], s, d, start=False, stop=True)
                    last.then_inc(S["sc_used"], 1)

            pe.wait_ge(S["warm_ready"], 1)
            for _ in range(WARM):
                pe.matmul(ps_o[:, 0:HALF], zeros[:, 0:P], zeros[:], start=True, stop=True)
            pe.wait_ge(S["ident_ready"], 1)
            turn(h0, S["h0_turned"], turned_banks[0], S["h0_ready"], 0)
            for c in range(DC):
                pe.wait_ge(ld_wkq[c // 2], 16)
                pe.wait_ge(S["h_t0"], c // 2 + 1)
                last = pe.matmul(ps_a[:], h_t[:, c, :], wkq[:, c, :], start=(c == 0), stop=(c == DC - 1))
            last.then_inc(S["kq_done"], 1)
            gate_sums(0)
            gate_sums(1)
            turn(kq, S["kq_turned"], [ps_x], S["kq_taken"], 0)
            gate_sums(2)
            pe.wait_ge(S["ld_wv"], 16)
            values(0)
            gate_sums(3)
            pe.wait_ge(S["kq_t_ready"], 1)
            pe.wait_ge(S["eq_ready"], 2)
            pe.wait_ge(S["ld_smalls"], 16)
            for c in range(2):
                pe.matmul(ps_c[:, 0:P], kq_t[:, 2 + c, :], kq_t[:, c, :], start=(c == 0), stop=(c == 1))
            for t in range(2):
                for c in range(2):
                    pe.matmul(ps_c[:, (1 + t) * P:(2 + t) * P], eq_b[:, c, t, :], kq_t[:, c, :], start=(c == 0), stop=(c == 1))
            for c in range(2):
                last = pe.matmul(ps_c[:, 3 * P:3 * P + 2], kq_t[:, 2 + c, :], smalls[:, EK + 2 * c:EK + 2 * c + 2],
                                 start=(c == 0), stop=(c == 1))
            last.then_inc(S["qk_done"], 1)
            for c in range(1, DC):
                last = values(c)
            last.then_inc(S["v_done"], 1)
            type_sums(0)
            pe.wait_ge(S["prob_ready"], 1)
            pe.transpose(ps_x[:, 0:P], prob[:], ident[:])
            pe.wait_ge(S["mass_ready"], 2)
            pe.transpose(ps_x[0:2, P:2 * P], gate_mass[:], ident[:]).then_inc(S["p_turned"], 1)
            type_sums(1)
            pe.wait_ge(S["p_t_ready"], 2)
            pe.wait_ge(S["v_taken"], 1)
            pe.wait_ge(S["ld_ev"], 16)
            for i in range(2):
                h = slice(i * HALF, (i + 1) * HALF)
                pe.matmul(m_banks[i][:, 0:HALF], prob_t[:], v_sb[:, h], start=True, stop=False)
                pe.matmul(m_banks[i][:, 0:HALF], mass_t[:], ev[:, h], start=False, stop=True).then_inc(S["m_done"], 1)
            for c in range(2, 5):
                type_sums(c)
            turn(cen, S["turned"], turned_banks[0], S["cen_ready"], 0)
            for c in range(5, EC - RING):
                type_sums(c)
            for i in range(2):
                for c in range(EC - RING, EC):
                    type_sums(c, [i])

            def split_dense(out, k, l, done, cols=slice(0, D), start=True):
                w = slot[k % SLOTS]
                pe.wait_ge(hi_ready, 2 * (k + 1))
                lo_wait(pe, k)
                for i in range(2):
                    pe.wait_ge(S["h_hi"], 2 * l + i + 1)
                    for c in (2 * i, 2 * i + 1):
                        for j in range(2):
                            pe.matmul(out, h_hl[:, 0, c, :], w[:, j, c, cols], start=start and c == 0 and j == 0, stop=False)
                    pe.wait_ge(S["h_lo"], 2 * l + i + 1)
                    for c in (2 * i, 2 * i + 1):
                        last = pe.matmul(out, h_hl[:, 1, c, :], w[:, 0, c, cols], start=False, stop=(c == DC - 1))
                last.then_inc(done, 1)

            def bases(l):
                for b in range(BASES):
                    if l == 1 or b >= 2:
                        pe.wait_ge(S["hb_lo"], BASES * l + b - 1)
                    split_dense((ps_a, ps_b)[b % 2][:], (BASES + 1) * l + b, l, S["w_used"])

            def aggregate(l, done):
                for i in range(2):
                    h = slice(i * HALF, (i + 1) * HALF)
                    for b in range(BASES):
                        pe.wait_ge(S["hb_lo"], BASES * l + b + 1)
                        pe.wait_ge(S["adj_lo"], 2 * l + b // 2 + 1)
                        a, m = adj_hl[l], hb_hl
                        out = agg_banks[i][:, 0:HALF]
                        pe.matmul(out, a[:, 0, b, :], m[:, 0, b, h], start=(b == 0), stop=False)
                        pe.matmul(out, a[:, 0, b, :], m[:, 1, b, h], start=False, stop=False)
                        last = pe.matmul(out, a[:, 1, b, :], m[:, 0, b, h], start=False, stop=(b == BASES - 1))
                    last.then_inc(done, 1)

            bases(0)
            split_dense(ps_c[:], 4, 0, S["w_used"])
            aggregate(0, S["agg_done"])
            turn(h1, S["turned"], turned_banks[1], S["h1_ready"], 0)
            pe.wait_ge(S["norm_row_ready"], 1)
            pe.transpose(ps_sc[:, P:2 * P], norm_row, ident[:]).then_inc(S["norm_turned"], 1)
            bases(1)
            split_dense(ps_c[:], 9, 1, S["w_used"])
            aggregate(1, S["conv_done"])
            pe.wait_ge(S["adj_sum"], 3)
            pe.wait_ge(S["norm_t_ready"], 1)
            pe.transpose(ps_sc[:, 0:P], t_sb[:, 0, :], ident[:])
            pe.transpose(ps_sc[:, 2 * P:3 * P], norm_t, ident[:]).then_inc(S["later_turned"], 1)

            def gather(n):
                pe.wait_ge(S["scaled_ready"], n - 1)
                for c in range(DC):
                    pe.wait_ge(S["cen_ready"], 2 * n - 1 + c // 2)
                    last = pe.matmul(z_banks[c // 2][:, (c % 2) * P:(c % 2 + 1) * P], cen[:, c * P:(c + 1) * P], scaled[:, n - 2, :],
                                     start=True, stop=True)
                    if c % 2:
                        last.then_inc(S["z_done"], 1)

            def keep_warm(n, bank):
                for _ in range(n):
                    pe.matmul(bank[:, 0:HALF], zeros[:, 0:P], zeros[:], start=True, stop=True)

            pe.wait_ge(S["ones_ready"], 1)
            pe.wait_ge(S["ld_bias2"], 16)
            pe.wait_ge(S["ld_u"], 16)
            pe.wait_ge(S["ld_vt"], 16)
            for i in range(2):
                pe.matmul(l2_banks[i][:, 0:HALF], ones[:], bias2[:, i * HALF:(i + 1) * HALF], start=True, stop=False)
            keep_warm(8, z_banks[0])
            gather(2)
            for c in range(DC):
                pe.wait_ge(S["z_taken"], c // 2 + 1)
                last = pe.matmul(ps_c[0:RANK, 0:P], u_w[:, c, :], z_t[:, c, :], start=(c == 0), stop=(c == DC - 1))
            last.then_inc(S["low_done"], 1)
            pe.wait_ge(S["low_taken"], 1)
            for i in range(2):
                h = slice(i * HALF, (i + 1) * HALF)
                pe.matmul(l2_banks[i][:, 0:HALF], low[:], vt_w[:, h], start=False, stop=True).then_inc(S["l2_done"], 1)
            pe.wait_ge(S["norm_ready"], 1)
            pe.wait_ge(S["ld_bias_b"], 48)
            for i in range(2):
                pe.matmul(l3_banks[i][:, 0:HALF], norm_adj[:], bias_b[:, 2, i * HALF:(i + 1) * HALF], start=True, stop=False)
            keep_warm(10, ps_sc)
            gather(3)
            for i in range(2):
                split_dense(l3_banks[i][:, 0:HALF], TILES, 2, S["l3_done"], cols=slice(i * HALF, (i + 1) * HALF), start=False)


def kernel(**inputs):
    import numpy as np
    import concourse.bacc as bacc
    from concourse.bass_utils import run_bass_kernel_spmd

    i = {k: np.asarray(v) for k, v in inputs.items()}

    def rows(a):
        return np.broadcast_to(a.reshape(1, -1), (P, a.size))

    def halves(a):
        return a.reshape(2, 2, P).transpose(2, 1, 0).reshape(P, 4)

    pad = np.zeros((P, 1), np.float32)
    pad[:RANK, 0] = i["L2_gnn_s"]
    arrays = {
        "x": i["x"],
        "ints": np.stack([i[k].reshape(P, EC) for k in ("src", "dst", "edge_type_8")], axis=1),
        "smalls": np.concatenate([
            i["edge_weight"].reshape(P, EC), i["edge_weight1"].reshape(P, EC), halves(i["L0_gnn_Ek"]), halves(i["L0_gnn_Eq"]),
            rows(i["L0_gnn_idx_bias"]), rows(i["L0_gnn_idx_mult"]), rows(i["L1_gnn_comp0"]), rows(i["L1_gnn_comp1"]), pad], axis=1),
        "biases": np.stack([i["L1_gnn_bias0"], i["L1_gnn_bias1"], i["L3_gnn_b"], i["L2_gnn_bias"]]),
        "ev": i["L0_gnn_Ev"],
        "wkq": np.concatenate([i["L0_gnn_Wk"], i["L0_gnn_Wq"]], axis=1),
        "wv": i["L0_gnn_Wv"],
        "conv": np.concatenate([i["L1_gnn_basis0"], i["L1_gnn_loop0"][None], i["L1_gnn_basis1"], i["L1_gnn_loop1"][None]]),
        "u": i["L2_gnn_U"],
        "vt": i["L2_gnn_Vt"],
        "w3": i["L3_gnn_W"].T,
    }
    nc = bacc.Bacc("TRN2", target_bir_lowering=False, num_devices=1)
    args, maps = [], {}
    for name, a in arrays.items():
        a = np.ascontiguousarray(a)
        maps[f"in_{name}"] = a
        args.append(nc.dram_tensor(f"in_{name}", a.shape, mybir.dt.from_np(a.dtype), kind="ExternalInput").ap())
    args.append(nc.dram_tensor("out_0", (P, D), F32, kind="ExternalOutput").ap())
    gnn_stack(nc, *args)
    r = run_bass_kernel_spmd(nc, [maps], core_ids=[0])
    return r.results[0]["out_0"]
```
